# Optimizing a Trainium2 kernel written in Bass

```python
import numpy as np
import jax
import jax.numpy as jnp

def _softmax(x, axis=-1):
    return jax.nn.softmax(x, axis=axis)
def _gelu(x):
    return jax.nn.gelu(x, approximate=True)
def _silu(x):
    return jax.nn.silu(x)
def _sigmoid(x):
    return jax.nn.sigmoid(x)
def _layernorm(x, axis=-1, eps=1e-5):
    m = jnp.mean(x, axis=axis, keepdims=True)
    v = jnp.var(x, axis=axis, keepdims=True)
    return (x - m) / jnp.sqrt(v + eps)
def _scatter_add(tgt, idx, src, axis=0):
    return tgt.at[idx].add(src)
def _segment_sum(src, seg, n):
    return jax.ops.segment_sum(src, seg, n)

kernel_name = 'mk_conv_preact_d4_conv_nchw16_29c659'

def setup_inputs(seed: int = 0):
    np.random.seed(seed)
    _w = jnp.asarray
    def _rec_inputs():
        import jax
        import jax.numpy as jnp
        _gk = jax.random.key(seed)
        x = -7.109e-05 + 0.9999 * jax.random.normal(jax.random.fold_in(_gk, 1), (1, 16, 2048, 2048), jnp.float32)
        return x
    x = _rec_inputs()
    def _L0_conv_setup():
        import jax, jax.numpy as jnp
        import numpy as np
        N = 2048
        IN_DIM = 16
        OUT_DIM = 16

        def _set_partitions(items):
            if not items:
                yield []
                return
            first, rest = (items[0], items[1:])
            for part in _set_partitions(rest):
                for i in range(len(part)):
                    yield (part[:i] + [part[i] + [first]] + part[i + 1:])
                yield ([[first]] + part)

        def _partitions():
            items = [('i', 0), ('i', 1), ('o', 0), ('o', 1)]
            parts = []
            for p in _set_partitions(items):
                blocks = []
                for blk in p:
                    iset = sorted((d for t, d in blk if t == 'i'))
                    oset = sorted((d for t, d in blk if t == 'o'))
                    blocks.append((iset, oset))
                parts.append(blocks)
            return parts
        PARTITIONS = _partitions()

        def _basis_apply(X, W, blocks, eye_n, ones_n):
            blk_letters = 'ijkl'
            in_sub = [''] * 2
            for bi, (iset, oset) in enumerate(blocks):
                for d in iset:
                    in_sub[d] = blk_letters[bi]
            subs = ['bc' + ''.join(in_sub)]
            ops = [X]
            fresh = iter('uvwxyz')
            out_letter = [''] * 2
            denom = 1.0
            for bi, (iset, oset) in enumerate(blocks):
                if not oset:
                    denom *= float(N)
                    continue
                if iset:
                    base = blk_letters[bi]
                else:
                    base = next(fresh)
                    subs.append(base)
                    ops.append(ones_n)
                out_letter[oset[0]] = base
                for od in oset[1:]:
                    l2 = next(fresh)
                    subs.append(base + l2)
                    ops.append(eye_n)
                    out_letter[od] = l2
            subs.append('co')
            ops.append(W)
            expr = ','.join(subs) + '->bo' + ''.join(out_letter)
            return jnp.einsum(expr, *ops) / denom
        key = jax.random.key(seed)
        k1, k2 = jax.random.split(key)
        stdv = 0.1 / np.sqrt(IN_DIM)
        X = jax.random.normal(k1, (1, IN_DIM, N, N), dtype=jnp.float32)
        weights = jax.random.uniform(k2, (len(PARTITIONS), IN_DIM, OUT_DIM), minval=-stdv, maxval=stdv, dtype=jnp.float32)
        bias = jnp.ones((len(PARTITIONS),), dtype=jnp.float32)
        return {'X': X, 'weights': weights, 'bias': bias}
    _L0_conv_all = _L0_conv_setup()
    _L0_conv_in = {k: v for k, v in _L0_conv_all.items() if k in ('weights', 'bias', )}
    del _L0_conv_all

    def _L1_conv_setup():
        import jax, jax.numpy as jnp
        import numpy as np
        N = 2048
        IN_DIM = 16
        OUT_DIM = 16

        def _set_partitions(items):
            if not items:
                yield []
                return
            first, rest = (items[0], items[1:])
            for part in _set_partitions(rest):
                for i in range(len(part)):
                    yield (part[:i] + [part[i] + [first]] + part[i + 1:])
                yield ([[first]] + part)

        def _partitions():
            items = [('i', 0), ('i', 1), ('o', 0), ('o', 1)]
            parts = []
            for p in _set_partitions(items):
                blocks = []
                for blk in p:
                    iset = sorted((d for t, d in blk if t == 'i'))
                    oset = sorted((d for t, d in blk if t == 'o'))
                    blocks.append((iset, oset))
                parts.append(blocks)
            return parts
        PARTITIONS = _partitions()

        def _basis_apply(X, W, blocks, eye_n, ones_n):
            blk_letters = 'ijkl'
            in_sub = [''] * 2
            for bi, (iset, oset) in enumerate(blocks):
                for d in iset:
                    in_sub[d] = blk_letters[bi]
            subs = ['bc' + ''.join(in_sub)]
            ops = [X]
            fresh = iter('uvwxyz')
            out_letter = [''] * 2
            denom = 1.0
            for bi, (iset, oset) in enumerate(blocks):
                if not oset:
                    denom *= float(N)
                    continue
                if iset:
                    base = blk_letters[bi]
                else:
                    base = next(fresh)
                    subs.append(base)
                    ops.append(ones_n)
                out_letter[oset[0]] = base
                for od in oset[1:]:
                    l2 = next(fresh)
                    subs.append(base + l2)
                    ops.append(eye_n)
                    out_letter[od] = l2
            subs.append('co')
            ops.append(W)
            expr = ','.join(subs) + '->bo' + ''.join(out_letter)
            return jnp.einsum(expr, *ops) / denom
        key = jax.random.key(seed)
        k1, k2 = jax.random.split(key)
        stdv = 0.1 / np.sqrt(IN_DIM)
        X = jax.random.normal(k1, (1, IN_DIM, N, N), dtype=jnp.float32)
        weights = jax.random.uniform(k2, (len(PARTITIONS), IN_DIM, OUT_DIM), minval=-stdv, maxval=stdv, dtype=jnp.float32)
        bias = jnp.ones((len(PARTITIONS),), dtype=jnp.float32)
        return {'X': X, 'weights': weights, 'bias': bias}
    _L1_conv_all = _L1_conv_setup()
    _L1_conv_in = {k: v for k, v in _L1_conv_all.items() if k in ('weights', 'bias', )}
    del _L1_conv_all

    def _L2_conv_setup():
        import jax, jax.numpy as jnp
        import numpy as np
        N = 2048
        IN_DIM = 16
        OUT_DIM = 16

        def _set_partitions(items):
            if not items:
                yield []
                return
            first, rest = (items[0], items[1:])
            for part in _set_partitions(rest):
                for i in range(len(part)):
                    yield (part[:i] + [part[i] + [first]] + part[i + 1:])
                yield ([[first]] + part)

        def _partitions():
            items = [('i', 0), ('i', 1), ('o', 0), ('o', 1)]
            parts = []
            for p in _set_partitions(items):
                blocks = []
                for blk in p:
                    iset = sorted((d for t, d in blk if t == 'i'))
                    oset = sorted((d for t, d in blk if t == 'o'))
                    blocks.append((iset, oset))
                parts.append(blocks)
            return parts
        PARTITIONS = _partitions()

        def _basis_apply(X, W, blocks, eye_n, ones_n):
            blk_letters = 'ijkl'
            in_sub = [''] * 2
            for bi, (iset, oset) in enumerate(blocks):
                for d in iset:
                    in_sub[d] = blk_letters[bi]
            subs = ['bc' + ''.join(in_sub)]
            ops = [X]
            fresh = iter('uvwxyz')
            out_letter = [''] * 2
            denom = 1.0
            for bi, (iset, oset) in enumerate(blocks):
                if not oset:
                    denom *= float(N)
                    continue
                if iset:
                    base = blk_letters[bi]
                else:
                    base = next(fresh)
                    subs.append(base)
                    ops.append(ones_n)
                out_letter[oset[0]] = base
                for od in oset[1:]:
                    l2 = next(fresh)
                    subs.append(base + l2)
                    ops.append(eye_n)
                    out_letter[od] = l2
            subs.append('co')
            ops.append(W)
            expr = ','.join(subs) + '->bo' + ''.join(out_letter)
            return jnp.einsum(expr, *ops) / denom
        key = jax.random.key(seed)
        k1, k2 = jax.random.split(key)
        stdv = 0.1 / np.sqrt(IN_DIM)
        X = jax.random.normal(k1, (1, IN_DIM, N, N), dtype=jnp.float32)
        weights = jax.random.uniform(k2, (len(PARTITIONS), IN_DIM, OUT_DIM), minval=-stdv, maxval=stdv, dtype=jnp.float32)
        bias = jnp.ones((len(PARTITIONS),), dtype=jnp.float32)
        return {'X': X, 'weights': weights, 'bias': bias}
    _L2_conv_all = _L2_conv_setup()
    _L2_conv_in = {k: v for k, v in _L2_conv_all.items() if k in ('weights', 'bias', )}
    del _L2_conv_all

    def _L3_conv_setup():
        import jax, jax.numpy as jnp
        import numpy as np
        N = 2048
        IN_DIM = 16
        OUT_DIM = 16

        def _set_partitions(items):
            if not items:
                yield []
                return
            first, rest = (items[0], items[1:])
            for part in _set_partitions(rest):
                for i in range(len(part)):
                    yield (part[:i] + [part[i] + [first]] + part[i + 1:])
                yield ([[first]] + part)

        def _partitions():
            items = [('i', 0), ('i', 1), ('o', 0), ('o', 1)]
            parts = []
            for p in _set_partitions(items):
                blocks = []
                for blk in p:
                    iset = sorted((d for t, d in blk if t == 'i'))
                    oset = sorted((d for t, d in blk if t == 'o'))
                    blocks.append((iset, oset))
                parts.append(blocks)
            return parts
        PARTITIONS = _partitions()

        def _basis_apply(X, W, blocks, eye_n, ones_n):
            blk_letters = 'ijkl'
            in_sub = [''] * 2
            for bi, (iset, oset) in enumerate(blocks):
                for d in iset:
                    in_sub[d] = blk_letters[bi]
            subs = ['bc' + ''.join(in_sub)]
            ops = [X]
            fresh = iter('uvwxyz')
            out_letter = [''] * 2
            denom = 1.0
            for bi, (iset, oset) in enumerate(blocks):
                if not oset:
                    denom *= float(N)
                    continue
                if iset:
                    base = blk_letters[bi]
                else:
                    base = next(fresh)
                    subs.append(base)
                    ops.append(ones_n)
                out_letter[oset[0]] = base
                for od in oset[1:]:
                    l2 = next(fresh)
                    subs.append(base + l2)
                    ops.append(eye_n)
                    out_letter[od] = l2
            subs.append('co')
            ops.append(W)
            expr = ','.join(subs) + '->bo' + ''.join(out_letter)
            return jnp.einsum(expr, *ops) / denom
        key = jax.random.key(seed)
        k1, k2 = jax.random.split(key)
        stdv = 0.1 / np.sqrt(IN_DIM)
        X = jax.random.normal(k1, (1, IN_DIM, N, N), dtype=jnp.float32)
        weights = jax.random.uniform(k2, (len(PARTITIONS), IN_DIM, OUT_DIM), minval=-stdv, maxval=stdv, dtype=jnp.float32)
        bias = jnp.ones((len(PARTITIONS),), dtype=jnp.float32)
        return {'X': X, 'weights': weights, 'bias': bias}
    _L3_conv_all = _L3_conv_setup()
    _L3_conv_in = {k: v for k, v in _L3_conv_all.items() if k in ('weights', 'bias', )}
    del _L3_conv_all

    return {
        "x": x,
        "L0_conv_weights": _L0_conv_in["weights"],
        "L0_conv_bias": _L0_conv_in["bias"],
        "L1_conv_weights": _L1_conv_in["weights"],
        "L1_conv_bias": _L1_conv_in["bias"],
        "L2_conv_weights": _L2_conv_in["weights"],
        "L2_conv_bias": _L2_conv_in["bias"],
        "L3_conv_weights": _L3_conv_in["weights"],
        "L3_conv_bias": _L3_conv_in["bias"],
    }

def reference(x, L0_conv_weights, L0_conv_bias, L1_conv_weights, L1_conv_bias, L2_conv_weights, L2_conv_bias, L3_conv_weights, L3_conv_bias):
    import jax
    import jax.numpy as jnp
    def _L0_conv_ref(X, weights, bias):
        import jax, jax.numpy as jnp
        import numpy as np
        N = 2048
        IN_DIM = 16
        OUT_DIM = 16

        def _set_partitions(items):
            if not items:
                yield []
                return
            first, rest = (items[0], items[1:])
            for part in _set_partitions(rest):
                for i in range(len(part)):
                    yield (part[:i] + [part[i] + [first]] + part[i + 1:])
                yield ([[first]] + part)

        def _partitions():
            items = [('i', 0), ('i', 1), ('o', 0), ('o', 1)]
            parts = []
            for p in _set_partitions(items):
                blocks = []
                for blk in p:
                    iset = sorted((d for t, d in blk if t == 'i'))
                    oset = sorted((d for t, d in blk if t == 'o'))
                    blocks.append((iset, oset))
                parts.append(blocks)
            return parts
        PARTITIONS = _partitions()

        def _basis_apply(X, W, blocks, eye_n, ones_n):
            blk_letters = 'ijkl'
            in_sub = [''] * 2
            for bi, (iset, oset) in enumerate(blocks):
                for d in iset:
                    in_sub[d] = blk_letters[bi]
            subs = ['bc' + ''.join(in_sub)]
            ops = [X]
            fresh = iter('uvwxyz')
            out_letter = [''] * 2
            denom = 1.0
            for bi, (iset, oset) in enumerate(blocks):
                if not oset:
                    denom *= float(N)
                    continue
                if iset:
                    base = blk_letters[bi]
                else:
                    base = next(fresh)
                    subs.append(base)
                    ops.append(ones_n)
                out_letter[oset[0]] = base
                for od in oset[1:]:
                    l2 = next(fresh)
                    subs.append(base + l2)
                    ops.append(eye_n)
                    out_letter[od] = l2
            subs.append('co')
            ops.append(W)
            expr = ','.join(subs) + '->bo' + ''.join(out_letter)
            return jnp.einsum(expr, *ops) / denom
        eye_n = jnp.eye(N, dtype=X.dtype)
        ones_n = jnp.ones((N,), dtype=X.dtype)
        Y = None
        for i, blocks in enumerate(PARTITIONS):
            Yi = _basis_apply(X, weights[i], blocks, eye_n, ones_n)
            Y = Yi if Y is None else Y + Yi
        return Y + jnp.sum(bias)

    def _L1_conv_ref(X, weights, bias):
        import jax, jax.numpy as jnp
        import numpy as np
        N = 2048
        IN_DIM = 16
        OUT_DIM = 16

        def _set_partitions(items):
            if not items:
                yield []
                return
            first, rest = (items[0], items[1:])
            for part in _set_partitions(rest):
                for i in range(len(part)):
                    yield (part[:i] + [part[i] + [first]] + part[i + 1:])
                yield ([[first]] + part)

        def _partitions():
            items = [('i', 0), ('i', 1), ('o', 0), ('o', 1)]
            parts = []
            for p in _set_partitions(items):
                blocks = []
                for blk in p:
                    iset = sorted((d for t, d in blk if t == 'i'))
                    oset = sorted((d for t, d in blk if t == 'o'))
                    blocks.append((iset, oset))
                parts.append(blocks)
            return parts
        PARTITIONS = _partitions()

        def _basis_apply(X, W, blocks, eye_n, ones_n):
            blk_letters = 'ijkl'
            in_sub = [''] * 2
            for bi, (iset, oset) in enumerate(blocks):
                for d in iset:
                    in_sub[d] = blk_letters[bi]
            subs = ['bc' + ''.join(in_sub)]
            ops = [X]
            fresh = iter('uvwxyz')
            out_letter = [''] * 2
            denom = 1.0
            for bi, (iset, oset) in enumerate(blocks):
                if not oset:
                    denom *= float(N)
                    continue
                if iset:
                    base = blk_letters[bi]
                else:
                    base = next(fresh)
                    subs.append(base)
                    ops.append(ones_n)
                out_letter[oset[0]] = base
                for od in oset[1:]:
                    l2 = next(fresh)
                    subs.append(base + l2)
                    ops.append(eye_n)
                    out_letter[od] = l2
            subs.append('co')
            ops.append(W)
            expr = ','.join(subs) + '->bo' + ''.join(out_letter)
            return jnp.einsum(expr, *ops) / denom
        eye_n = jnp.eye(N, dtype=X.dtype)
        ones_n = jnp.ones((N,), dtype=X.dtype)
        Y = None
        for i, blocks in enumerate(PARTITIONS):
            Yi = _basis_apply(X, weights[i], blocks, eye_n, ones_n)
            Y = Yi if Y is None else Y + Yi
        return Y + jnp.sum(bias)

    def _L2_conv_ref(X, weights, bias):
        import jax, jax.numpy as jnp
        import numpy as np
        N = 2048
        IN_DIM = 16
        OUT_DIM = 16

        def _set_partitions(items):
            if not items:
                yield []
                return
            first, rest = (items[0], items[1:])
            for part in _set_partitions(rest):
                for i in range(len(part)):
                    yield (part[:i] + [part[i] + [first]] + part[i + 1:])
                yield ([[first]] + part)

        def _partitions():
            items = [('i', 0), ('i', 1), ('o', 0), ('o', 1)]
            parts = []
            for p in _set_partitions(items):
                blocks = []
                for blk in p:
                    iset = sorted((d for t, d in blk if t == 'i'))
                    oset = sorted((d for t, d in blk if t == 'o'))
                    blocks.append((iset, oset))
                parts.append(blocks)
            return parts
        PARTITIONS = _partitions()

        def _basis_apply(X, W, blocks, eye_n, ones_n):
            blk_letters = 'ijkl'
            in_sub = [''] * 2
            for bi, (iset, oset) in enumerate(blocks):
                for d in iset:
                    in_sub[d] = blk_letters[bi]
            subs = ['bc' + ''.join(in_sub)]
            ops = [X]
            fresh = iter('uvwxyz')
            out_letter = [''] * 2
            denom = 1.0
            for bi, (iset, oset) in enumerate(blocks):
                if not oset:
                    denom *= float(N)
                    continue
                if iset:
                    base = blk_letters[bi]
                else:
                    base = next(fresh)
                    subs.append(base)
                    ops.append(ones_n)
                out_letter[oset[0]] = base
                for od in oset[1:]:
                    l2 = next(fresh)
                    subs.append(base + l2)
                    ops.append(eye_n)
                    out_letter[od] = l2
            subs.append('co')
            ops.append(W)
            expr = ','.join(subs) + '->bo' + ''.join(out_letter)
            return jnp.einsum(expr, *ops) / denom
        eye_n = jnp.eye(N, dtype=X.dtype)
        ones_n = jnp.ones((N,), dtype=X.dtype)
        Y = None
        for i, blocks in enumerate(PARTITIONS):
            Yi = _basis_apply(X, weights[i], blocks, eye_n, ones_n)
            Y = Yi if Y is None else Y + Yi
        return Y + jnp.sum(bias)

    def _L3_conv_ref(X, weights, bias):
        import jax, jax.numpy as jnp
        import numpy as np
        N = 2048
        IN_DIM = 16
        OUT_DIM = 16

        def _set_partitions(items):
            if not items:
                yield []
                return
            first, rest = (items[0], items[1:])
            for part in _set_partitions(rest):
                for i in range(len(part)):
                    yield (part[:i] + [part[i] + [first]] + part[i + 1:])
                yield ([[first]] + part)

        def _partitions():
            items = [('i', 0), ('i', 1), ('o', 0), ('o', 1)]
            parts = []
            for p in _set_partitions(items):
                blocks = []
                for blk in p:
                    iset = sorted((d for t, d in blk if t == 'i'))
                    oset = sorted((d for t, d in blk if t == 'o'))
                    blocks.append((iset, oset))
                parts.append(blocks)
            return parts
        PARTITIONS = _partitions()

        def _basis_apply(X, W, blocks, eye_n, ones_n):
            blk_letters = 'ijkl'
            in_sub = [''] * 2
            for bi, (iset, oset) in enumerate(blocks):
                for d in iset:
                    in_sub[d] = blk_letters[bi]
            subs = ['bc' + ''.join(in_sub)]
            ops = [X]
            fresh = iter('uvwxyz')
            out_letter = [''] * 2
            denom = 1.0
            for bi, (iset, oset) in enumerate(blocks):
                if not oset:
                    denom *= float(N)
                    continue
                if iset:
                    base = blk_letters[bi]
                else:
                    base = next(fresh)
                    subs.append(base)
                    ops.append(ones_n)
                out_letter[oset[0]] = base
                for od in oset[1:]:
                    l2 = next(fresh)
                    subs.append(base + l2)
                    ops.append(eye_n)
                    out_letter[od] = l2
            subs.append('co')
            ops.append(W)
            expr = ','.join(subs) + '->bo' + ''.join(out_letter)
            return jnp.einsum(expr, *ops) / denom
        eye_n = jnp.eye(N, dtype=X.dtype)
        ones_n = jnp.ones((N,), dtype=X.dtype)
        Y = None
        for i, blocks in enumerate(PARTITIONS):
            Yi = _basis_apply(X, weights[i], blocks, eye_n, ones_n)
            Y = Yi if Y is None else Y + Yi
        return Y + jnp.sum(bias)

    def _gn(v, G=8, eps=1e-5):
        B_, C_, H_, W_ = v.shape
        g = v.reshape(B_, G, C_ // G, H_, W_)
        m = jnp.mean(g, axis=(2, 3, 4), keepdims=True)
        s = jnp.var(g, axis=(2, 3, 4), keepdims=True)
        return ((g - m) / jnp.sqrt(s + eps)).reshape(v.shape)

    def _ln_c(v, eps=1e-6):
        m = jnp.mean(v, axis=1, keepdims=True)
        s = jnp.var(v, axis=1, keepdims=True)
        return (v - m) / jnp.sqrt(s + eps)

    def _ln_t(v, eps=1e-5):
        m = jnp.mean(v, axis=-1, keepdims=True)
        s = jnp.var(v, axis=-1, keepdims=True)
        return (v - m) / jnp.sqrt(s + eps)

    def _to_tokens(v):
        B_, C_, H_, W_ = v.shape
        return v.reshape(B_, C_, H_ * W_).transpose(0, 2, 1)
    def _from_tokens(t, like):
        B_, C_, H_, W_ = like.shape
        return t.transpose(0, 2, 1).reshape(B_, C_, H_, W_)

    x = x + _L0_conv_ref(_gn(x), L0_conv_weights, L0_conv_bias)
    x = x + _L1_conv_ref(_gn(x), L1_conv_weights, L1_conv_bias)
    x = x + _L2_conv_ref(_gn(x), L2_conv_weights, L2_conv_bias)
    x = x + _L3_conv_ref(_gn(x), L3_conv_weights, L3_conv_bias)
    return x


_drawn_inputs = setup_inputs


def setup_inputs(seed=0):
    import zlib

    import numpy as np

    out = dict(_drawn_inputs(seed))
    spreads = {'L0_conv_bias': (1.0, 0.6),
     'L1_conv_bias': (1.0, 0.6),
     'L2_conv_bias': (1.0, 0.6),
     'L3_conv_bias': (1.0, 0.6)}
    factors = {'x': 3.076,
     'L0_conv_weights': 23.978,
     'L1_conv_weights': 28.017,
     'L2_conv_weights': 30.364,
     'L3_conv_weights': 31.144}
    for name, (base, spread) in spreads.items():
        noise = np.random.default_rng([zlib.crc32(name.encode()), seed]).standard_normal(out[name].shape)
        drawn = base * np.exp(spread * noise) if base else spread * noise
        out[name] = jnp.asarray(drawn.astype(out[name].dtype))
    for name, factor in factors.items():
        out[name] = (out[name] * factor).astype(out[name].dtype)
    return out
```

```python
from collections import namedtuple
from contextlib import ExitStack

import numpy as np
import concourse.bass as bass
from concourse import mybir

LAYERS = 4
CH = 16
BLK = 128
SUB = 8
GRP = BLK // SUB
CG = GRP // 4
GW = BLK + GRP
LOOK = 3
SLOTS = 4
ROWS = 6 * CH
FEATS = 5 * CH
EPS = 1e-5
U_, V_, E_, B_, P_, Q_ = (slice(CH * k, CH * k + CH) for k in range(6))

(D_DIA, D_GAM, D_TRACE, D_RHO, D_TOTAL, R_DIA, SWAP, R_GAM, SAME, S_DIA, S_GAM, ALL_TRACE, R_RHO, S_RHO,
 ALL_TOTAL) = range(15)

Step = namedtuple("Step", "t i j k kind tail slot par off group prev")
Step.__doc__ = """One mirrored pair of blocks (i, j) and (j, i).
t: its number; kind: 'diag' (i == j) or 'off'; k: (j - i) mod blocks; tail: the last steps, k = blocks / 2;
slot, par: load buffer and parity; off: off-diagonal steps before it; group: number of its column block j in order of use."""


def main_step(j, k, nb, prev=None):
    spj = nb // 2
    return Step(j * spj + k, (j + nb - k) % nb, j, k, "off" if k else "diag", False, k % SLOTS, k % 2,
                j * (spj - 1) + max(k - 1, 0), j, prev)


def tail_step(q, nb, prev=None):
    spj = nb // 2
    return Step(nb * spj + q, q + spj, q, spj, "off", True, q % SLOTS, q % 2, nb * (spj - 1) + q, nb + q, prev)


def walk(eng, nb, step):
    spj = nb // 2
    step(main_step(0, 0, nb))

    def column(j):
        for k in range(1, spj):
            step(main_step(j, k, nb, main_step(j, k - 1, nb)))

    column(0)
    step(main_step(1, 0, nb, main_step(0, spj - 1, nb)))
    with eng.Fori(1, nb - 1) as j:
        column(j)
        step(main_step(j + 1, 0, nb, main_step(j, spj - 1, nb)))
    column(nb - 1)
    for q in range(spj):
        step(tail_step(q, nb, tail_step(q - 1, nb) if q else main_step(nb - 1, spj - 1, nb)))


def ahead(s, nb):
    spj = nb // 2
    if s.tail:
        return tail_step(s.j + LOOK, nb) if s.j + LOOK < spj else None
    if s.k + LOOK < spj:
        return main_step(s.j, s.k + LOOK, nb)
    if isinstance(s.j, int) and s.j == nb - 1:
        return tail_step(s.k + LOOK - spj, nb)
    return main_step(s.j + 1, s.k + LOOK - spj, nb)


def constants(n):
    eye = np.eye
    ca = np.arange(BLK)
    sub = (ca[:, None] % SUB == np.arange(SUB)).astype(np.float32)
    chan = (ca[:, None] // SUB == np.arange(CH)).astype(np.float32)
    r, o = np.arange(ROWS)[:, None], np.arange(ROWS)[None]
    same_group = (r % CH) // 2 == (o % CH) // 2
    energy = np.array([.5, .5, .5 / n, -.5 / n, .5, .5])
    centre = np.array([.5, 0, .5 / n, -.5 / n, 0, 0])
    f = np.arange(FEATS)
    part = np.arange(BLK)

    def gram_place(first):
        m = np.zeros((BLK, FEATS))
        m[:, first:first + CH] = chan / (4. * n * n)
        return m

    def channel_spread(first):
        m = np.zeros((FEATS, BLK))
        m[first:first + CH] = chan.T / 2
        return m

    pieces = {
        "ident": eye(BLK),
        "sub": sub,
        "half_chan": chan / 2,
        "mean": np.full((BLK, BLK), 1. / n),
        "gram_s": gram_place(3 * CH),
        "gram_t": gram_place(4 * CH),
        "feat_scale": np.broadcast_to(np.where(f < 3 * CH, 1. / n, -2. / n), (BLK, FEATS)),
        "blocks": ((f[:, None] // CH == f // CH) & (f >= 3 * CH)) | ((f[:, None] < 3 * CH) & (f < 3 * CH)),
        "energy": same_group * energy[r // CH],
        "energy_mean": same_group * centre[r // CH],
        "centre": same_group * centre[r // CH] * (o < 4 * CH),
        "state": np.concatenate([eye(CH, FEATS), eye(CH, FEATS, CH), eye(CH, FEATS, 2 * CH), eye(CH, FEATS, 2 * CH),
                                 eye(CH, FEATS, 3 * CH), eye(CH, FEATS, 4 * CH)]),
        "state_t": np.concatenate([eye(CH, FEATS), eye(CH, FEATS, CH), eye(CH, FEATS, 2 * CH), eye(CH, FEATS, 2 * CH),
                                   eye(CH, FEATS, 3 * CH), eye(CH, FEATS, 4 * CH)]).T,
        "spread_p": channel_spread(3 * CH),
        "spread_q": channel_spread(4 * CH),
        "sub_pairs": np.broadcast_to(eye(SUB).reshape(1, -1), (BLK, SUB * SUB)),
        "keep_mid": np.where((part % 64) // CH >= 1, -1., 0.)[:, None],
        "keep_low": np.where((part % 64) // CH >= 2, -1., 0.)[:, None],
        "onehot": np.broadcast_to(eye(GRP).reshape(1, -1), (BLK, GRP * GRP)),
    }
    where, at = {}, 0
    blob = np.zeros((BLK, sum(v.shape[1] for v in pieces.values())), np.float32)
    for name, v in pieces.items():
        blob[:v.shape[0], at:at + v.shape[1]] = v
        where[name] = (v.shape[0], at, v.shape[1])
        at += v.shape[1]
    pick_channel = np.tile(np.repeat(eye(CH), SUB, axis=1), (3, 1))
    pick_group = np.tile(np.repeat(eye(GRP), BLK, axis=1), (3, 1))
    return blob, where, pick_channel, pick_group


def build(nc, x, weights, biases, const_f32, const_channel, const_group, out, where):
    F32, BF16 = mybir.dt.float32, mybir.dt.bfloat16
    ALU, ACT, AX = mybir.AluOpType, mybir.ActivationFunctionType, mybir.AxisListType
    n = x.shape[2]
    nb = n // BLK
    spj = nb // 2
    steps = nb * spj + spj
    offs = nb * (spj - 1) + spj
    groups = 2 * nb + spj
    ds = bass.ds

    x_rows = x.rearrange("z c (i a) (j b) -> (z i) a c j b", a=BLK, b=BLK)
    x_chan = x.rearrange("z c (i a g) (j b) -> (z c) i a g j b", a=SUB, b=BLK, g=GRP)
    out_rows = out.rearrange("z c (i a) (j b) -> (z i) a c j b", a=BLK, b=BLK)
    out_chan = out.rearrange("z c (i a g) (j b) -> (z c) i a g j b", a=SUB, b=BLK, g=GRP)

    ctx = ExitStack()
    with ctx:
        def sb(name, shape, dt=F32):
            return ctx.enter_context(nc.sbuf_tensor(name, shape, dt))

        def sem(name):
            return ctx.enter_context(nc.semaphore(name))

        TILE = CH * BLK
        xt = sb("xt", [BLK, SLOTS, TILE])
        yt = sb("yt", [BLK, SLOTS, TILE])
        st0 = sb("st0", [BLK, 2, GRP, GW])
        late = sb("late", [BLK, 6 * TILE])
        const = sb("const", [BLK, const_f32.shape[1]])
        both_slots = sb("both_slots", [BLK, max(2 * steps * CH, 2 * n)])
        row_slots = both_slots[:, 0:steps * CH]
        col_slots = both_slots[:, steps * CH:2 * steps * CH]
        shared = sb("shared", [BLK, 2, 4 * BLK])
        jsum, t_sb = shared[:, :, 0:nb * GRP], shared
        gram = sb("gram", [BLK, 2, BLK])
        dia = sb("dia", [BLK, nb, CH])
        lowrank = sb("lowrank", [112, 2, n], BF16)
        colterm = sb("colterm", [48, 2, n], BF16)
        moving = sb("moving", [112, 2 * 2 * GRP * BLK], BF16)
        wt = sb("wt", [CH, LAYERS, 15, CH])
        bias_sb = sb("bias_sb", [1, LAYERS, 15])
        beta = sb("beta", [1, LAYERS])
        brow = sb("brow", [1, LAYERS, ROWS])
        step_m = sb("step_m", [97, LAYERS, ROWS])
        step_mean = sb("step_mean", [97, LAYERS, ROWS])
        state = sb("state", [ROWS, FEATS + 1])
        state_t = sb("state_t", [FEATS, ROWS])
        mean_row = sb("mean_row", [1, ROWS])
        m80 = sb("m80", [1, 2, FEATS])
        m_col = sb("m_col", [FEATS, 1])
        normed = sb("normed", [97, FEATS + 1])
        means = sb("means", [BLK, 3 * CH])
        rs = sb("rs", [BLK, 2, FEATS])
        phi = sb("phi", [FEATS, FEATS])
        prod = sb("prod", [ROWS, FEATS])
        col = sb("col", [ROWS, 8])
        kron = sb("kron", [BLK, 2, CH, SUB])
        coef = sb("coef", [FEATS, 3, CH])
        coef_b = sb("coef_b", [FEATS, 2, 3, CH])
        krow = sb("krow", [1, 2, 3, CH])
        kd_row = sb("kd_row", [1, CH, SUB])
        ones = sb("ones", [1, 256])
        st1 = late[:, 0:2 * GRP * GW].rearrange("p (s g w) -> p s g w", s=2, g=GRP)
        f1 = late[:, 0:nb * FEATS].rearrange("p (i f) -> p i f", f=FEATS)
        f1s = late[:, nb * FEATS:2 * nb * FEATS].rearrange("p (i f) -> p i f", f=FEATS)
        parts = late[0:112, 0:n].bitcast(BF16).rearrange("p (s n) -> p s n", s=2)
        at_b = 2 * GRP * GW
        wsize = LAYERS * 6 * ROWS
        place = [late[0:CH, at_b + m * wsize:at_b + (m + 1) * wsize].rearrange("p (l r o) -> p l r o", l=LAYERS, r=6)
                 for m in range(2)]
        spread = late[:, at_b:at_b + 2 * nb * GRP * SUB].rearrange("p (s v a) -> p s v a", s=2, a=SUB)
        terms = both_slots[0:112, 0:2 * n].rearrange("p (s n) -> p s n", s=2)
        at_c = at_b + 2 * wsize
        coef_d = late[0:FEATS, 3 * TILE:3 * TILE + SUB * BLK].rearrange("f (k c a) -> f k c a", k=SUB, c=CH)
        dterm = late[:, 5 * TILE:5 * TILE + n].rearrange("p (v a) -> p v a", a=SUB)
        masked = late[:, at_c:at_c + TILE]
        f2 = late[0:FEATS, 0:3 * n].rearrange("f (i a r g) -> f i a r g", a=SUB, r=3, g=GRP)
        wtmp = late[0:CH, at_c + TILE:at_c + TILE + 4 * LAYERS * CH].rearrange("p (k l o) -> p k l o", k=4, l=LAYERS)
        at_i = at_c + TILE + 4 * LAYERS * CH
        row_i, col_i = (late[:, at_i + m * nb * CH:at_i + (m + 1) * nb * CH].rearrange("p (i c) -> p i c", c=CH)
                        for m in range(2))
        gtmp = late[:, at_c:at_c + 2 * BLK].rearrange("p (k w) -> p k w", k=2)
        junk = [(shared[:, ch // 4, 256 + 64 * (ch % 4):320 + 64 * (ch % 4)] if ch < 8
                 else late[:, at_i + 64 * (ch - 8):at_i + 64 * (ch - 7)]).bitcast(BF16) for ch in range(CH)]
        st = [st0, st1]
        out_ij = [late[:, b * TILE:(b + 1) * TILE].rearrange("p (g b) -> p g b", g=GRP) for b in range(2)]
        out_ji = [late[:, (2 + b) * TILE:(3 + b) * TILE].rearrange("p (c a) -> p c a", c=CH) for b in range(2)]
        out_jit = late[:, 4 * TILE:5 * TILE].rearrange("p (q w) -> p q w", q=4)
        ps = ctx.enter_context(nc.psum_tensor("ps", [BLK, 8, 512], F32))

        def c(name):
            rows, at, width = where[name]
            return const[0:rows, at:at + width]

        ident, sub = c("ident"), c("sub")

        x_in = [sem(f"x_in{s}") for s in range(SLOTS)]
        y_in = [sem(f"y_in{s}") for s in range(SLOTS)]
        const_in, weights_in, lowrank_in = sem("const_in"), sem("weights_in"), sem("lowrank_in")
        onehot_set, zeroed = sem("onehot_set"), sem("zeroed")
        place_done, matrices_in, beta_done = sem("place_done"), sem("matrices_in"), sem("beta_done")
        yt_ready, yt_used, st_ready = sem("yt_ready"), sem("yt_used"), sem("st_ready")
        gram_step, gram_used = sem("gram_step"), sem("gram_used")
        rows_done, dia_masked, dia_done = sem("rows_done"), sem("dia_masked"), sem("dia_done")
        pool_own, dve_own = sem("pool_own"), sem("dve_own")
        rows_folded = sem("rows_folded")
        to_pe, from_pe = sem("to_pe"), sem("from_pe")
        f2_ready, f2_done, root_in, root_out = sem("f2_ready"), sem("f2_done"), sem("root_in"), sem("root_out")
        terms_ready = sem("terms_ready")
        terms_b, terms_a = sem("terms_b"), sem("terms_a")
        colterm_done, middle_done = sem("colterm_done"), sem("middle_done")
        yt2_ready, yt2_used, moving_ready = sem("yt2_ready"), sem("yt2_used"), sem("moving_ready")
        tmix_ready, mix_ready, t_copied, out_done = sem("tmix_ready"), sem("mix_ready"), sem("t_copied"), sem("out_done")
        diag_own = sem("diag_own")
        jit_turned, ji_copied = sem("jit_turned"), sem("ji_copied")
        ij_stored = [sem(f"ij_stored{b}") for b in range(2)]
        ji_stored = [sem(f"ji_stored{b}") for b in range(2)]

        def wait(eng, s, value):
            if not (isinstance(value, int) and value <= 0):
                eng.wait_ge(s, value)

        pass1_loads = steps // SLOTS

        def slot_turn(s):
            return s.t // SLOTS if isinstance(s.t, int) else s.j * (spj // SLOTS) + s.k // SLOTS

        def par_turn(s):
            return s.t // 2 if isinstance(s.t, int) else s.j * (spj // 2) + s.k // 2

        def ji_before(s):
            if s.tail:
                return nb * (spj // 2 - 1 + s.par) + s.j // 2
            return s.j * (spj // 2 - 1 + s.par) + (s.k - 1) // 2

        def gram_index(s):
            return nb * 2 + s.j if s.tail else 2 * s.j + (s.kind == "off")

        moved_sums = [row_slots[:, k * nb * GRP:(k + 1) * nb * GRP] for k in range(2)]

        block = ctx.enter_context(nc.Block())

        @block.sync
        def _(sp):
            sp.dma_start(const[:, :], const_f32).then_inc(const_in, 16)

            def held(v):
                if not isinstance(v, int):
                    sp.compute_val(v)
                return v

            def load1(s):
                sp.dma_start(yt[:, s.slot].rearrange("p (c b) -> p c b", c=CH),
                             x_rows[s.j, :, :, s.i, :]).then_inc(y_in[s.slot], 16)
                sp.dma_start(xt[:, s.slot].rearrange("p (c b) -> p c b", c=CH),
                             x_rows[s.i, :, :, s.j, :]).then_inc(x_in[s.slot], 16)

            def load2(s):
                sp.dma_start(yt[:, s.slot].rearrange("p (c b) -> p c b", c=CH),
                             x_rows[s.j, :, :, s.i, :]).then_inc(y_in[s.slot], 16)
                for a in range(SUB):
                    sp.dma_start(xt[a:BLK:SUB, s.slot].rearrange("p (g b) -> p g b", g=GRP),
                                 x_chan[:, s.i, a, :, s.j, :]).then_inc(x_in[s.slot], 16)

            first = [main_step(0, k, nb) for k in range(LOOK)]
            for s in first:
                load1(s)
            for layer in range(LAYERS):
                sp.dma_start(wt[:, layer], weights[layer].rearrange("k c o -> c k o")).then_inc(weights_in, 16)
                sp.dma_start(bias_sb[:, layer], biases[layer].rearrange("(z k) -> z k", z=1)).then_inc(weights_in, 16)
            sp.wait_ge(zeroed, 1)
            for p in range(2):
                for i in range(nb):
                    sp.dma_start(lowrank[0:48, p, i * BLK:(i + 1) * BLK], const_channel).then_inc(lowrank_in, 16)
                for q in range(2):
                    sp.dma_start(moving[64:112, (2 * p + q) * TILE:(2 * p + q + 1) * TILE],
                                 const_group).then_inc(lowrank_in, 16)

            def pass1(s):
                nxt = ahead(s, nb)
                if nxt:
                    nxt = nxt._replace(i=held(nxt.i), j=held(nxt.j))
                t, turned = held(s.t), held(2 * s.t)
                masked_count = held(s.prev.j + 1) if s.prev and s.prev.kind == "diag" else 0
                wait(sp, dia_masked, masked_count)
                wait(sp, st_ready, t)
                wait(sp, rows_done, t)
                wait(sp, yt_ready, turned)
                if nxt:
                    load1(nxt)
                else:
                    load2(first[s.t + LOOK - steps])

            walk(sp, nb, pass1)
            sp.wait_ge(place_done, 1)
            for m, dst in enumerate((step_m, step_mean)):
                for rb in range(6):
                    sp.dma_start(dst[rb * CH:(rb + 1) * CH], place[m][:, :, rb, :]).then_inc(matrices_in, 16)
            sp.wait_ge(beta_done, 1)
            sp.dma_start(step_mean[96:97], brow[:, :, :]).then_inc(matrices_in, 16)

            def store_ji(s):
                if s.kind == "off":
                    i, j = held(s.i), held(s.j)
                    wait(sp, ji_copied, held(4 * s.off + 4))
                    sp.dma_start(out_rows[j, :, :, i, :], out_ji[s.par]).then_inc(ji_stored[s.par], 16)

            def pass2(s):
                nxt = ahead(s, nb)
                if not s.prev:
                    sp.wait_ge(st_ready, steps)
                    sp.wait_ge(rows_done, steps)
                    sp.wait_ge(yt_ready, 2 * steps)
                if nxt:
                    nxt = nxt._replace(i=held(nxt.i), j=held(nxt.j))
                    wait(sp, yt2_used, held(4 * s.t))
                    load2(nxt)
                if s.prev:
                    store_ji(s.prev)

            walk(sp, nb, pass2)
            store_ji(tail_step(spj - 1, nb))
            for b in range(2):
                sp.wait_ge(ij_stored[b], 16 * SUB * steps // 2)
                sp.wait_ge(ji_stored[b], 16 * (nb * (spj // 2 - 1 + b) + spj // 2))

        @block.gpsimd
        def _(pool):
            own = [0]

            def link(ins):
                own[0] += 1
                ins.then_inc(pool_own, 1)
                pool.wait_ge(pool_own, own[0])

            pool.wait_ge(const_in, 16)
            for b in range(2):
                for k in range(2):
                    last = nc.gpsimd.tensor_copy(st[b][:, k, :, BLK:GW],
                                                 c("onehot").rearrange("p (g w) -> p g w", g=GRP))
            last.then_inc(onehot_set, 1)
            nc.gpsimd.memset(lowrank[:, :, :], 0.0)
            nc.gpsimd.memset(moving[:, :], 0.0).then_inc(zeroed, 1)

            def masked_diagonal(s):
                pool.wait_ge(x_in[s.slot], 16 * (slot_turn(s) + 1))
                wait(pool, dia_done, s.j)
                nc.gpsimd.tensor_tensor(masked.rearrange("p (c b) -> p c b", c=CH),
                                        xt[:, s.slot].rearrange("p (c b) -> p c b", c=CH),
                                        ident.unsqueeze(1).to_broadcast([BLK, CH, BLK]),
                                        ALU.mult).then_inc(dia_masked, 1)

            masked_diagonal(main_step(0, 0, nb))

            pool.wait_ge(weights_in, 16 * 2 * LAYERS)
            coefs, mean_coefs = place

            def w(k):
                return wt[:, :, k, :]

            def put(dst, a, b, op=ALU.add):
                link(nc.gpsimd.tensor_tensor(dst, a, b, op))

            def neg(dst, a):
                link(nc.gpsimd.tensor_scalar(dst, a, -1.0, None, ALU.mult))

            link(nc.gpsimd.memset(coefs, 0.0))
            link(nc.gpsimd.memset(mean_coefs, 0.0))
            UR, VR, ER, BR, PR, QR = range(6)
            for rb, (r, s_, d, on_u, on_v) in ((UR, (R_RHO, S_RHO, D_RHO, SAME, SWAP)),
                                               (VR, (R_GAM, S_GAM, D_GAM, SWAP, SAME))):
                put(coefs[:, :, rb, U_], w(r), w(on_u))
                put(coefs[:, :, rb, V_], w(s_), w(on_v))
                put(coefs[:, :, rb, B_], w(r), w(s_))
                put(coefs[:, :, rb, E_], coefs[:, :, rb, B_], w(d))
            tr, ts, td, tk = (wtmp[:, k] for k in range(4))
            for tmp, a, b in ((tr, R_RHO, R_GAM), (ts, S_RHO, S_GAM), (td, D_RHO, D_GAM)):
                put(tmp, w(a), w(b))
            link(nc.gpsimd.tensor_scalar(wtmp[:, 0:3], wtmp[:, 0:3], 1.0 / n, None, ALU.mult))
            link(nc.gpsimd.tensor_scalar(tk, w(ALL_TOTAL), 1.0 / n, None, ALU.mult))
            eb = coefs[:, :, ER]
            bb = coefs[:, :, BR]
            put(eb[:, :, U_], w(R_DIA), tr)
            put(eb[:, :, V_], w(S_DIA), ts)
            put(eb[:, :, B_], eb[:, :, U_], eb[:, :, V_])
            put(eb[:, :, E_], eb[:, :, B_], w(D_DIA))
            put(eb[:, :, E_], eb[:, :, E_], td)
            put(coefs[:, :, PR, P_], w(SAME), w(SWAP))
            put(coefs[:, :, QR, Q_], w(SAME), w(SWAP), ALU.subtract)
            both = coefs[:, :, PR, P_]
            put(eb[:, :, E_], eb[:, :, E_], both)
            neg(bb[:, :, U_], tr)
            neg(bb[:, :, V_], ts)
            put(bb[:, :, E_], bb[:, :, U_], bb[:, :, V_])
            put(bb[:, :, B_], bb[:, :, E_], both)
            put(bb[:, :, E_], bb[:, :, E_], td, ALU.subtract)
            link(nc.gpsimd.tensor_copy(mean_coefs, coefs))
            mb = mean_coefs

            def more(rb, cols, a, op=ALU.add):
                put(mb[:, :, rb, cols], mb[:, :, rb, cols], a, op)

            for rb, r, s_ in ((UR, R_RHO, S_RHO), (VR, R_GAM, S_GAM), (ER, R_DIA, S_DIA)):
                more(rb, U_, w(s_))
                more(rb, V_, w(r))
            for cols in (U_, V_, E_, B_):
                more(UR, cols, w(ALL_TOTAL))
                more(ER, cols, w(ALL_TRACE))
                more(ER, cols, tk)
                more(BR, cols, tk, ALU.subtract)
            more(UR, E_, w(D_TOTAL))
            more(ER, E_, w(D_TRACE))
            more(ER, U_, ts)
            more(ER, V_, tr)
            more(BR, U_, ts, ALU.subtract)
            more(BR, V_, tr, ALU.subtract)
            link(nc.gpsimd.tensor_scalar(td, w(D_TOTAL), 1.0 / n, None, ALU.mult))
            more(ER, E_, td)
            own[0] += 1
            nc.gpsimd.tensor_tensor(mb[:, :, BR, E_], mb[:, :, BR, E_], td, ALU.subtract).then_inc(pool_own, 1)
            pool.wait_ge(pool_own, own[0])
            nc.gpsimd.memset(col[:, 7:8], 0.0).then_inc(place_done, 1)

            with pool.Fori(1, nb) as j:
                masked_diagonal(main_step(j, 0, nb))

            pool.wait_ge(rows_done, steps)
            slots = row_slots[:, 0:nb * spj * CH].rearrange("p (j k c) -> p j k c", j=nb, k=spj)
            tail = row_slots[:, nb * spj * CH:].rearrange("p (j c) -> p j c", c=CH)
            link(nc.gpsimd.tensor_copy(row_i, slots[:, :, 0]))
            for k in range(1, spj):
                nc.gpsimd.tensor_tensor(row_i[:, 0:nb - k], row_i[:, 0:nb - k], slots[:, k:nb, k], ALU.add)
                link(nc.gpsimd.tensor_tensor(row_i[:, nb - k:nb], row_i[:, nb - k:nb], slots[:, 0:k, k], ALU.add))
            nc.gpsimd.tensor_tensor(row_i[:, spj:nb], row_i[:, spj:nb], tail, ALU.add).then_inc(rows_folded, 1)

            pool.wait_ge(from_pe, 1)
            link(nc.gpsimd.memset(terms, 0.0))
            nc.gpsimd.memset(col[:, 6:7], 0.0).then_inc(terms_ready, 1)

            def store_ij(s):
                pool.wait_ge(out_done, 4 * s.t + 4)
                for a in range(SUB):
                    pool.dma_start(out_chan[:, s.i, a, :, s.j, :],
                                   out_ij[s.par][a:BLK:SUB]).then_inc(ij_stored[s.par], 16)

            walk(pool, nb, store_ij)

        @block.scalar
        def _(act):
            def row_sums(s):
                act.wait_ge(x_in[s.slot], 16 * (slot_turn(s) + 1))
                wait(act, rows_done, s.t)
                for ch in range(CH):
                    last = nc.scalar.activation(junk[ch], xt[:, s.slot, ch * BLK:(ch + 1) * BLK], ACT.Copy,
                                                accum_out=row_slots[:, ds(s.t * CH + ch, 1)])
                last.then_inc(rows_done, 1)

            walk(act, nb, row_sums)

            act.wait_ge(f2_ready, 1)
            for b in range(n // 512):
                for r in range(3):
                    last = nc.scalar.activation(f2[:, 4 * b:4 * b + 4, :, r].rearrange("f i a g -> f (i a) g"),
                                                ps[0:FEATS, 4 + b].rearrange("f (v g) -> f v g", g=GRP), ACT.Copy)
            last.then_inc(f2_done, 1)
            for layer in range(LAYERS):
                act.wait_ge(root_in, layer + 1)
                nc.scalar.activation(col[:, 4:5], col[:, 3:4], ACT.Sqrt).then_inc(root_out, 1)
            act.wait_ge(terms_ready, 1)
            for b in range(nb // 2):
                act.wait_ge(terms_b, b + 1)
                last = nc.scalar.activation(terms[0:48, :, b * 256:(b + 1) * 256],
                                            ps[0:48, b].rearrange("p (s n) -> p s n", s=2), ACT.Copy)
                last.then_inc(terms_a, 1)

            def column_terms(m, j):
                base = (m % 2) * (2 * TILE)
                for k in range(2):
                    last = nc.scalar.activation(
                        moving[0:48, ds(base + k * TILE, TILE)].rearrange("p (g b) -> p g b", g=GRP),
                        colterm[:, k, ds(j * BLK, BLK)].unsqueeze(1).to_broadcast([48, GRP, BLK]), ACT.Copy)
                last.then_inc(moving_ready, 1)

            def more_terms(s):
                if s.tail and 0 < s.j < spj - 1:
                    act.wait_ge(mix_ready, 4 * s.t)
                    column_terms(nb + s.j + 1, s.j + 1)
                elif s.tail and s.j == 0:
                    act.wait_ge(mix_ready, 4 * s.t)
                    column_terms(nb + 1, 1)
                elif s.k == 1 and not (isinstance(s.j, int) and s.j == 0):
                    act.wait_ge(mix_ready, 4 * spj * s.j)
                    if isinstance(s.j, int):
                        column_terms(nb, 0)
                    else:
                        column_terms(s.j + 1, s.j + 1)

            def copy_t(s, q):
                idx = 4 * s.t + q
                act.wait_ge(tmix_ready, idx + 1)
                wait(act, out_done, idx - 1)
                nc.scalar.activation(t_sb[:, q % 2], ps[:, 4 + q % 2], ACT.Copy).then_inc(t_copied, 1)

            def copy_ji(s, q):
                if s.kind == "diag":
                    return
                act.wait_ge(jit_turned, 4 * s.off + q + 1)
                wait(act, ji_stored[s.par], 16 * ji_before(s))
                nc.scalar.activation(
                    out_ji[s.par].rearrange("p c (a g) -> p g c a", g=GRP)[:, CG * q:CG * q + CG],
                    ps[:, 6 + q % 2].rearrange("p (g c a) -> p g c a", g=CG, c=CH), ACT.Copy).then_inc(ji_copied, 1)

            def pass2(s):
                for q in range(4):
                    if q or s.prev:
                        copy_t(s if q else s.prev, (q - 1) % 4)
                    if q == 3 or s.prev:
                        copy_ji(s if q == 3 else s.prev, (q - 3) % 4)
                    if q == 0:
                        more_terms(s)

            act.wait_ge(middle_done, 1)
            act.wait_ge(lowrank_in, 16 * (2 * nb + 4))
            act.wait_ge(colterm_done, 1)
            column_terms(0, 0)
            column_terms(1, 1)
            walk(act, nb, pass2)
            last_step = tail_step(spj - 1, nb)
            copy_t(last_step, 3)
            for q in range(1, 4):
                copy_ji(last_step, q)
        @block.vector
        def _(dve):
            own = [0]

            def link(ins):
                own[0] += 1
                ins.then_inc(dve_own, 1)
                dve.wait_ge(dve_own, own[0])

            tt = nc.vector.tensor_tensor
            link(nc.vector.memset(gram[:, :, :], 0.0))
            dve.wait_ge(onehot_set, 1)

            def form(s):
                dve.wait_ge(x_in[s.slot], 16 * (slot_turn(s) + 1))
                wait(dve, gram_step, s.t - 1)
                for h in range(2):
                    dve.wait_ge(yt_ready, 2 * s.t + h + 1)
                    blk = xt[:, s.slot, h * 1024:(h + 1) * 1024].rearrange("p (c g b) -> p c g b", c=8, g=GRP)
                    mir = ps[:, 2 * h:2 * h + 2].rearrange("p k (c g b) -> p (k c) g b", c=4, g=GRP)
                    for k, op in enumerate((ALU.add, ALU.subtract)):
                        dst = st[s.par][:, k, :, 0:BLK].rearrange("p g (c b) -> p c g b", c=CH)[:, 8 * h:8 * h + 8]
                        last = tt(dst, blk, mir, op)
                    if h:
                        last.then_inc(st_ready, 1)
                    nc.vector.tensor_reduce(col_slots[:, ds(s.t * CH + 8 * h, 8)],
                                            ps[:, 2 * h:2 * h + 2].rearrange("p k (c b) -> p (k c) b", c=4),
                                            AX.X, ALU.add).then_inc(yt_used, 1)

            def take_gram(s):
                g = gram_index(s)
                dve.wait_ge(gram_step, s.t + 1)
                wait(dve, gram_used, g)
                bank = 4 + 2 * (s.par if s.tail else (s.kind == "off"))
                last = nc.vector.scalar_tensor_tensor(gram[:, :, :], ps[:, bank:bank + 2, 0:BLK],
                                                      1.0 if s.kind == "diag" else 2.0, gram[:, :, :],
                                                      ALU.mult, ALU.add)
                if s.kind == "off":
                    part = ps[:, bank:bank + 2, BLK:GW]
                    dst = jsum[:, :, ds(s.j * GRP, GRP)]
                    last = tt(dst, part, dst, ALU.add) if s.tail else nc.vector.tensor_copy(dst, part)
                last.then_inc(gram_used, 1)

            def ends_group(s):
                return s.kind == "diag" or s.tail or s.k == spj - 1

            def pass1(s):
                form(s)
                if s.prev and ends_group(s.prev):
                    take_gram(s.prev)
                if s.k == 2 and not s.tail:
                    dve.wait_ge(dia_masked, s.j + 1)
                    nc.vector.tensor_reduce(dia[:, ds(s.j, 1), :].rearrange("p i c -> p (i c)"),
                                            masked.rearrange("p (c b) -> p c b", c=CH),
                                            AX.X, ALU.add).then_inc(dia_done, 1)

            walk(dve, nb, pass1)

            dve.wait_ge(yt_used, 2 * steps)
            dve.wait_ge(rows_done, steps)
            slots = col_slots[:, 0:nb * spj * CH].rearrange("p (j k c) -> p j k c", j=nb, k=spj)
            tail = col_slots[:, nb * spj * CH:].rearrange("p (j c) -> p j c", c=CH)
            link(nc.vector.tensor_copy(col_i, slots[:, :, 0]))
            for k in range(1, spj):
                tt(col_i[:, 0:nb - k], col_i[:, 0:nb - k], slots[:, k:nb, k], ALU.add)
                link(tt(col_i[:, nb - k:nb], col_i[:, nb - k:nb], slots[:, 0:k, k], ALU.add))
            link(tt(col_i[:, spj:nb], col_i[:, spj:nb], tail, ALU.add))
            dve.wait_ge(weights_in, 16 * 2 * LAYERS)
            link(nc.vector.tensor_reduce(beta[:, :], bias_sb[:, :, :], AX.X, ALU.add))
            link(nc.vector.memset(brow[:, :, :], 0.0))
            nc.vector.tensor_copy(brow[:, :, 0:4 * CH],
                                  beta[:, :].unsqueeze(2).to_broadcast([1, LAYERS, 4 * CH])).then_inc(beta_done, 1)
            take_gram(tail_step(spj - 1, nb))
            dve.wait_ge(gram_used, groups)

            link(nc.vector.memset(rs[:, :, :], 0.0))
            link(nc.vector.memset(normed[:, :], 0.0))
            nc.vector.memset(normed[96:97, FEATS:FEATS + 1], 1.0)
            nc.vector.memset(ones[:, :], 1.0)
            nc.vector.memset(m80[:, :, :], 0.0)
            link(nc.vector.memset(mean_row[:, :], 0.0))
            dve.wait_ge(matrices_in, 16 * 13)
            dve.wait_ge(rows_folded, 1)
            width = nb * GRP
            for k, op in enumerate((ALU.subtract, ALU.add)):
                v = moved_sums[k]
                link(tt(v, jsum[:, 0], jsum[:, 1], op))
                last = tt(spread[:, k], v.unsqueeze(2).to_broadcast([BLK, width, SUB]),
                          sub.unsqueeze(1).to_broadcast([BLK, width, SUB]), ALU.mult)
            last.then_inc(to_pe, 1)
            for k in range(2):
                g3 = gtmp[:, k].rearrange("p (c a) -> p c a", c=CH)
                link(tt(g3, gram[:, k].rearrange("p (c a) -> p c a", c=CH),
                        sub.unsqueeze(1).to_broadcast([BLK, CH, SUB]), ALU.mult))
                link(nc.vector.tensor_reduce(rs[:, k, (3 + k) * CH:(4 + k) * CH], g3, AX.X, ALU.add))
            dve.wait_ge(from_pe, 1)
            for k, own_side in enumerate((row_i, col_i)):
                link(tt(f1[:, :, k * CH:(k + 1) * CH], own_side[:, :, :],
                        ps[:, k, 0:nb * CH].rearrange("p (i c) -> p i c", c=CH), ALU.add))
            link(nc.vector.tensor_scalar(f1[:, :, 0:2 * CH], f1[:, :, 0:2 * CH], 1.0 / n, None, ALU.mult))
            dve.wait_ge(dia_done, nb)
            nc.vector.tensor_copy(f1[:, :, 2 * CH:3 * CH], dia[:, :, :]).then_inc(to_pe, 1)
            dve.wait_ge(to_pe, 2)
            dve.wait_ge(from_pe, 2)
            link(nc.vector.tensor_copy(means[:, :], ps[:, 2, 0:3 * CH]))
            for k in range(2):
                nc.vector.tensor_copy(mean_row[:, 2 * k * CH:2 * (k + 1) * CH].rearrange("p (r c) -> p r c", r=2),
                                      means[0:1, 2 * k * CH:(2 * k + 1) * CH].unsqueeze(1).to_broadcast([1, 2, CH]))
            nc.vector.tensor_copy(m80[:, 0, 3 * CH:4 * CH], means[0:1, 0:CH])
            nc.vector.tensor_scalar(m80[:, 1, 3 * CH:4 * CH], means[0:1, 0:CH], -1.0, None, ALU.mult)
            link(tt(f1[:, :, 0:3 * CH], f1[:, :, 0:3 * CH],
                    means[:, :].unsqueeze(1).to_broadcast([BLK, nb, 3 * CH]), ALU.subtract))
            tt(f1[:, :, 3 * CH:4 * CH], f1[:, :, 0:CH], f1[:, :, CH:2 * CH], ALU.add)
            link(tt(f1[:, :, 4 * CH:], f1[:, :, 0:CH], f1[:, :, CH:2 * CH], ALU.subtract))
            link(nc.vector.tensor_scalar(f1[:, :, 3 * CH:], f1[:, :, 3 * CH:], 0.5, None, ALU.mult))
            tt(f1s, f1, c("feat_scale").unsqueeze(1).to_broadcast([BLK, nb, FEATS]),
               ALU.mult).then_inc(to_pe, 1)
            link(nc.vector.tensor_copy(state[:, 0:FEATS], c("state")))
            link(nc.vector.tensor_copy(state_t[:, :], c("state_t")))
            dve.wait_ge(from_pe, 3)
            link(nc.vector.tensor_copy(state[:, FEATS:], ps[0:ROWS, 0, 0:1]))
            link(nc.vector.tensor_copy(m_col[:, :], ps[0:FEATS, 0, 1:2]))
            tt(phi[:, :], ps[0:FEATS, 3, 0:FEATS], c("blocks"), ALU.mult).then_inc(to_pe, 1)
            pe_in, pe_out = 4, 3
            for layer in range(LAYERS):
                dve.wait_ge(from_pe, pe_out + 1)
                link(tt(col[:, 0:1], state[:, FEATS:], ps[0:ROWS, 0, 0:1], ALU.subtract))
                link(tt(col[:, 1:2], col[:, 0:1], col[:, 0:1], ALU.mult))
                link(tt(prod[:, :], state[:, 0:FEATS], ps[0:ROWS, 1, 0:FEATS], ALU.mult))
                nc.vector.tensor_reduce(col[:, 2:3], prod[:, :], AX.X, ALU.add).then_inc(to_pe, 1)
                dve.wait_ge(from_pe, pe_out + 2)
                nc.vector.tensor_scalar(col[:, 3:4], ps[0:ROWS, 2, 0:1], EPS, None, ALU.add).then_inc(root_in, 1)
                dve.wait_ge(root_out, layer + 1)
                link(nc.vector.reciprocal(col[:, 5:6], col[:, 4:5]))
                link(tt(col[:, 2:3], col[:, 5:6], col[:, 5:6], ALU.mult))
                link(tt(col[:, 2:3], col[:, 2:3], col[:, 3:4], ALU.mult))
                link(nc.vector.tensor_scalar(col[:, 2:3], col[:, 2:3], -0.5, 1.5, ALU.mult, ALU.add))
                link(tt(col[:, 5:6], col[:, 5:6], col[:, 2:3], ALU.mult))
                nc.vector.tensor_scalar(normed[0:ROWS, 0:FEATS], state[:, 0:FEATS], col[:, 5:6], None, ALU.mult)
                tt(normed[0:ROWS, FEATS:], col[:, 0:1], col[:, 5:6], ALU.mult).then_inc(to_pe, 1)
                dve.wait_ge(from_pe, pe_out + 3)
                tt(state[:, :], state[:, :], ps[0:ROWS, 3, 0:FEATS + 1], ALU.add)
                tt(mean_row[:, :], mean_row[:, :], ps[0:1, 2, 256:256 + ROWS], ALU.add)
                tt(state_t[:, :], state_t[:, :], ps[0:FEATS, 0, 256:256 + ROWS], ALU.add).then_inc(to_pe, 1)
                pe_in, pe_out = pe_in + 3, pe_out + 3
            dve.wait_ge(to_pe, pe_in)
            link(tt(coef[:, 0], state_t[:, U_], state_t[:, V_], ALU.add))
            link(tt(coef[:, 1], state_t[:, U_], state_t[:, V_], ALU.subtract))
            link(nc.vector.tensor_scalar(coef[:, 0:2], coef[:, 0:2], 0.5, None, ALU.mult))
            tt(coef[:, 0:2], coef[:, 0:2], state_t[:, 4 * CH:].rearrange("p (k c) -> p k c", k=2), ALU.subtract)
            link(tt(coef[:, 2], state_t[:, E_], state_t[:, B_], ALU.subtract))
            nc.vector.tensor_copy(coef_b[:, 0], coef[:, 0].unsqueeze(1).to_broadcast([FEATS, 3, CH]))
            nc.vector.tensor_scalar(coef_b[:, 1], coef[:, 1].unsqueeze(1).to_broadcast([FEATS, 3, CH]),
                                    -1.0, None, ALU.mult)
            for a in range(SUB):
                tt(coef_d[:, a], coef[:, 2].unsqueeze(2).to_broadcast([FEATS, CH, SUB]),
                   c("sub_pairs")[0:FEATS, a * SUB:(a + 1) * SUB].unsqueeze(1).to_broadcast([FEATS, CH, SUB]), ALU.mult)
            link(tt(krow[:, 1, 0], mean_row[:, E_], mean_row[:, B_], ALU.subtract))
            nc.vector.tensor_copy(kd_row[:, :, :], krow[:, 1, 0].unsqueeze(2).to_broadcast([1, CH, SUB]))
            dve.wait_ge(from_pe, pe_out + 1)
            link(tt(krow[:, 1, 1], mean_row[:, U_], ps[0:1, 2, 0:CH], ALU.subtract))
            nc.vector.tensor_copy(krow[:, 0], krow[:, 1, 1].unsqueeze(1).to_broadcast([1, 3, CH]))
            for k in range(2):
                last = tt(kron[:, k], ps[:, k, 0:CH].unsqueeze(2).to_broadcast([BLK, CH, SUB]),
                          sub.unsqueeze(1).to_broadcast([BLK, CH, SUB]), ALU.mult)
            last.then_inc(to_pe, 1)
            dve.wait_ge(from_pe, pe_out + 2)
            tt(dterm, ps[:, 3, 0:width].unsqueeze(2).to_broadcast([BLK, width, SUB]),
               sub.unsqueeze(1).to_broadcast([BLK, width, SUB]), ALU.mult).then_inc(to_pe, 1)
            dve.wait_ge(terms_ready, 1)
            for b in range(nb // 2):
                dve.wait_ge(terms_b, b + 1)
                last = nc.vector.tensor_copy(terms[64:112, :, b * 256:(b + 1) * 256],
                                             ps[64:112, b].rearrange("p (s n) -> p s n", s=2))
            link(last)
            dve.wait_ge(terms_a, nb // 2)
            for keep in ("keep_mid", "keep_low"):
                link(nc.vector.tensor_copy(parts, terms))
                link(nc.vector.scalar_tensor_tensor(terms, parts, c(keep)[0:112], terms, ALU.mult, ALU.add))
            dve.wait_ge(lowrank_in, 16 * (2 * nb + 4))
            nc.vector.tensor_copy(colterm[:, :, :], terms[0:48]).then_inc(colterm_done, 1)
            nc.vector.tensor_copy(lowrank[64:112], terms[64:112]).then_inc(middle_done, 1)
            dve.wait_ge(middle_done, 1)
            dve.wait_ge(colterm_done, 1)

            def form2(s, q):
                idx = 4 * s.t + q
                if q == 0:
                    dve.wait_ge(x_in[s.slot], 16 * (pass1_loads + SUB * (slot_turn(s) + 1)))
                dve.wait_ge(yt2_ready, idx + 1)
                wait(dve, mix_ready, idx - 3)
                for k, op in enumerate((ALU.add, ALU.subtract)):
                    last = tt(st0[:, k, CG * q:CG * q + CG, 0:BLK],
                              xt[:, s.slot, q * 512:(q + 1) * 512].rearrange("p (g b) -> p g b", g=CG),
                              ps[:, q % 2].rearrange("p (g b) -> p g b", g=CG), op)
                last.then_inc(yt2_used, 1)

            def combine(s, q):
                idx = 4 * s.t + q
                dve.wait_ge(mix_ready, idx + 1)
                dve.wait_ge(t_copied, idx + 1)
                if q == 0:
                    wait(dve, ij_stored[s.par], 16 * SUB * par_turn(s))
                s_prod = ps[:, 2 + q % 2].rearrange("p (g b) -> p g b", g=CG)
                t_prod = t_sb[:, q % 2].rearrange("p (g b) -> p g b", g=CG)
                dst = out_ij[s.par][:, CG * q:CG * q + CG]
                first = tt(dst, s_prod, t_prod, ALU.add)
                if s.kind == "diag":
                    first.then_inc(diag_own, 1)
                    if q == 3:
                        wait(dve, jit_turned, 4 * s.off)
                    dve.wait_ge(diag_own, 4 * s.j + q + 1)
                    flat = late[:, s.par * TILE + CG * q * BLK:s.par * TILE + CG * (q + 1) * BLK]
                    for g in range(CG):
                        at = g * BLK + CG * q + g
                        span = flat[:, at:(g + 1) * BLK:GRP]
                        last = tt(span, span,
                                  dterm[:, ds(s.j * GRP + CG * q + g, 1), :].rearrange("p z a -> p (z a)"), ALU.add)
                else:
                    if s.k > 1:
                        dve.wait_ge(jit_turned, 4 * s.off + q - 3)
                    last = tt(out_jit[:, q].rearrange("p (g b) -> p g b", g=CG), s_prod, t_prod, ALU.subtract)
                last.then_inc(out_done, 1)

            def pass2(s):
                for q in range(4):
                    form2(s, q)
                    if q >= 2 or s.prev:
                        combine(s if q >= 2 else s.prev, (q - 2) % 4)

            walk(dve, nb, pass2)
            for q in (2, 3):
                combine(tail_step(spj - 1, nb), q)

        @block.tensor
        def _(pe):
            mm = nc.tensor.matmul
            pe.wait_ge(const_in, 16)

            def turn(s):
                pe.wait_ge(y_in[s.slot], 16 * (slot_turn(s) + 1))
                for h in range(2):
                    wait(pe, yt_used, 2 * s.t + h - 1)
                    for ch in range(8 * h, 8 * h + 8):
                        last = nc.tensor.transpose(ps[:, ch // 4, (ch % 4) * BLK:(ch % 4 + 1) * BLK],
                                                   yt[:, s.slot, ch * BLK:(ch + 1) * BLK], ident)
                    last.then_inc(yt_ready, 1)

            def grams(s):
                g = gram_index(s)
                opens = s.kind == "diag" or s.tail or s.k == 1
                closes = s.kind == "diag" or s.tail or s.k == spj - 1
                bank = 4 + 2 * (s.par if s.tail else (s.kind == "off"))
                pe.wait_ge(st_ready, s.t + 1)
                if opens and s.kind == "off":
                    pe.wait_ge(gram_used, g - 1)
                width = BLK if s.kind == "diag" else GW
                for k in range(2):
                    for grp in range(GRP):
                        last = mm(ps[:, bank + k, 0:width], st[s.par][:, k, grp, 0:BLK], st[s.par][:, k, grp, 0:width],
                                  start=opens and grp == 0, stop=closes and grp == GRP - 1)
                last.then_inc(gram_step, 1)

            def pass1(s):
                turn(s)
                if s.prev:
                    grams(s.prev)

            walk(pe, nb, pass1)
            grams(tail_step(spj - 1, nb))

            one = ones[0:1, 0:1]
            pe.wait_ge(gram_used, groups)
            pe.wait_ge(to_pe, 1)
            for k in range(2):
                for i in range(nb):
                    last = mm(ps[:, k, i * CH:(i + 1) * CH],
                              spread[:, k, i * GRP:(i + 1) * GRP].rearrange("p g a -> p (g a)"),
                              c("half_chan"), start=True, stop=True)
            last.then_inc(from_pe, 1)
            pe.wait_ge(to_pe, 2)
            for i in range(nb):
                last = mm(ps[:, 2, 0:3 * CH], c("mean"), f1[:, i, 0:3 * CH], start=i == 0, stop=i == nb - 1)
            last.then_inc(from_pe, 1)
            pe.wait_ge(to_pe, 3)
            mm(ps[0:ROWS, 0, 0:1], mean_row[:, :], one, start=True, stop=True)
            mm(ps[0:FEATS, 0, 1:2], m80[:, 0], one, start=True, stop=True)
            cov = ps[0:FEATS, 3, 0:FEATS]
            for i in range(nb):
                mm(cov, f1s[:, i], f1[:, i], start=i == 0, stop=False)
            mm(cov, c("gram_s"), rs[:, 0], start=False, stop=False)
            mm(cov, c("gram_t"), rs[:, 1], start=False, stop=False)
            mm(cov, m80[:, 1], m80[:, 0], start=False, stop=True).then_inc(from_pe, 1)
            for i in range(nb):
                last = nc.tensor.transpose(ps[0:FEATS, 4 + i // 4, (i % 4) * BLK:(i % 4 + 1) * BLK], f1[:, i], ident)
            last.then_inc(f2_ready, 1)
            pe_in = 4
            for layer in range(LAYERS):
                pe.wait_ge(to_pe, pe_in)
                mm(ps[0:ROWS, 0, 0:1], c("centre"), state[:, FEATS:], start=True, stop=True)
                mm(ps[0:ROWS, 1, 0:FEATS], state_t[:, :], phi[:, :], start=True, stop=True).then_inc(from_pe, 1)
                pe.wait_ge(to_pe, pe_in + 1)
                mm(ps[0:ROWS, 2, 0:1], c("energy"), col[:, 2:3], start=True, stop=False)
                mm(ps[0:ROWS, 2, 0:1], c("energy_mean"), col[:, 1:2], start=False, stop=True).then_inc(from_pe, 1)
                pe.wait_ge(to_pe, pe_in + 2)
                mm(ps[0:ROWS, 3, 0:FEATS], step_m[0:ROWS, layer], normed[0:ROWS, 0:FEATS], start=True, stop=True)
                mm(ps[0:ROWS, 3, FEATS:FEATS + 1], step_mean[:, layer], normed[:, FEATS:], start=True, stop=True)
                mm(ps[0:1, 2, 256:256 + ROWS], normed[:, FEATS:], step_mean[:, layer], start=True, stop=True)
                mm(ps[0:FEATS, 0, 256:256 + ROWS], normed[0:ROWS, 0:FEATS], step_m[0:ROWS, layer],
                   start=True, stop=True).then_inc(from_pe, 1)
                pe_in += 3
            pe.wait_ge(to_pe, pe_in)
            mm(ps[:, 0, 0:CH], c("spread_p"), state_t[:, P_], start=True, stop=True)
            mm(ps[:, 1, 0:CH], c("spread_q"), state_t[:, Q_], start=True, stop=True)
            mm(ps[0:1, 2, 0:CH], m_col[:, :], state_t[:, P_], start=True, stop=True).then_inc(from_pe, 1)
            pe.wait_ge(to_pe, pe_in + 1)
            pe.wait_ge(f2_done, 1)
            for a in range(SUB):
                mm(ps[:, 3, 0:nb * GRP], coef_d[:, a].rearrange("f c a -> f (c a)"), f2[:, :, a, 0],
                   start=a == 0, stop=False)
            mm(ps[:, 3, 0:nb * GRP], kd_row[:, :, :].rearrange("z c a -> z (c a)"), ones[:, 0:nb * GRP],
               start=False, stop=True).then_inc(from_pe, 1)
            pe.wait_ge(to_pe, pe_in + 2)
            for b in range(nb // 2):
                for k in range(2):
                    dst = ps[0:48, b, k * 256:(k + 1) * 256]
                    mm(dst, coef_b[:, k].rearrange("f r c -> f (r c)"), f2[:, 2 * b:2 * b + 2, :, 0].rearrange("f i a g -> f (i a) g"),
                       start=True, stop=k == 1)
                    if k == 0:
                        mm(dst, krow[:, 0].rearrange("z r c -> z (r c)"), ones[:, :], start=False, stop=True)
                for i2 in range(2):
                    dst = ps[64:112, b].rearrange("p (k i c a) -> p i a k c", k=2, i=2, c=CH)
                    for a in range(SUB):
                        last = mm(dst[:, i2, a], f2[:, 2 * b + i2, a].rearrange("f r g -> f (r g)"),
                                  coef[:, 0:2], start=True, stop=True)
                last.then_inc(terms_b, 1)
            pe.wait_ge(terms_a, nb // 2)
            pe.wait_ge(middle_done, 1)

            def turn2(s, q):
                if q == 0:
                    pe.wait_ge(y_in[s.slot], 16 * (pass1_loads + slot_turn(s) + 1))
                wait(pe, yt2_used, 4 * s.t + q - 1)
                rows = yt[:, s.slot].rearrange("p (v g) -> p g v", g=GRP)
                for g in range(CG):
                    last = nc.tensor.transpose(ps[:, q % 2, g * BLK:(g + 1) * BLK], rows[:, CG * q + g], ident)
                last.then_inc(yt2_ready, 1)

            def mix(s, q):
                idx = 4 * s.t + q
                pe.wait_ge(yt2_used, idx + 1)
                pe.wait_ge(moving_ready, s.group + 1)
                wait(pe, out_done, idx - 1)
                base = (s.group % 2) * (2 * TILE)
                for k, done in ((1, tmix_ready), (0, mix_ready)):
                    dst = ps[:, 2 + 2 * k + q % 2]
                    mm(dst, lowrank[:, k, ds(s.i * BLK, BLK)], moving[:, ds(base + k * TILE + q * 512, 512)],
                       start=True, stop=False)
                    mm(dst, kron[:, k].rearrange("p c a -> p (c a)"), st0[:, k, CG * q:CG * q + CG, 0:BLK],
                       start=False, stop=True).then_inc(done, 1)

            def turn_back(s, q):
                if s.kind == "diag":
                    if q == 3:
                        wait(pe, ji_copied, 4 * s.off)
                    return
                pe.wait_ge(out_done, 4 * s.t + q + 1)
                if s.k > 1 or q > 1:
                    pe.wait_ge(ji_copied, 4 * s.off + q - 1)
                for g in range(CG):
                    last = nc.tensor.transpose(ps[:, 6 + q % 2, g * BLK:(g + 1) * BLK],
                                               out_jit[:, q, g * BLK:(g + 1) * BLK], ident)
                last.then_inc(jit_turned, 1)

            def pass2(s):
                for q in range(4):
                    turn2(s, q)
                    if q or s.prev:
                        mix(s if q else s.prev, (q - 1) % 4)
                    if q == 3 or s.prev:
                        turn_back(s if q == 3 else s.prev, (q - 3) % 4)

            walk(pe, nb, pass2)
            last_step = tail_step(spj - 1, nb)
            mix(last_step, 3)
            for q in range(1, 4):
                turn_back(last_step, q)


def kernel(x, **inputs):
    import concourse.bacc as bacc
    from concourse.bass_utils import run_bass_kernel_spmd

    nc = bacc.Bacc("TRN2", target_bir_lowering=False, num_devices=1)
    arrays, aps = {}, {}

    def dram(name, a):
        arrays[name] = a
        aps[name] = nc.dram_tensor(name, a.shape, mybir.dt.from_np(a.dtype), kind="ExternalInput").ap()
        return aps[name]

    blob, where, pick_channel, pick_group = constants(x.shape[2])
    bf16 = mybir.dt.np(mybir.dt.bfloat16)
    xin = dram("x", np.ascontiguousarray(x))
    ws = [dram(f"weights{k}", np.ascontiguousarray(inputs[f"L{k}_conv_weights"])) for k in range(LAYERS)]
    bs = [dram(f"bias{k}", np.ascontiguousarray(inputs[f"L{k}_conv_bias"])) for k in range(LAYERS)]
    cf = dram("const_f32", blob)
    cc = dram("const_channel", pick_channel.astype(bf16))
    cg = dram("const_group", pick_group.astype(bf16))
    out = nc.dram_tensor("out", x.shape, mybir.dt.float32, kind="ExternalOutput").ap()
    build(nc, xin, ws, bs, cf, cc, cg, out, where)
    r = run_bass_kernel_spmd(nc, [arrays], core_ids=[0])
    return r.results[0]["out"]
```

```python
from collections import namedtuple
from contextlib import ExitStack

import numpy as np
import concourse.bass as bass
from concourse import mybir

LAYERS = 4
CH = 16
BLK = 128
SUB = 8
GRP = BLK // SUB
CG = GRP // 4
GW = BLK + GRP
LOOK = 3
SLOTS = 4
SP_STORES = 3
ROWS = 6 * CH
FEATS = 5 * CH
EPS = 1e-5
U_, V_, E_, B_, P_, Q_ = (slice(CH * k, CH * k + CH) for k in range(6))

(D_DIA, D_GAM, D_TRACE, D_RHO, D_TOTAL, R_DIA, SWAP, R_GAM, SAME, S_DIA, S_GAM, ALL_TRACE, R_RHO, S_RHO,
 ALL_TOTAL) = range(15)

Step = namedtuple("Step", "t i j k kind tail slot par off group prev")
Step.__doc__ = """One mirrored pair of blocks (i, j) and (j, i).
t: its number; kind: 'diag' (i == j) or 'off'; k: (j - i) mod blocks; tail: the last steps, k = blocks / 2;
slot, par: load buffer and parity; off: off-diagonal steps before it; group: number of its column block j in order of use."""


def main_step(j, k, nb, prev=None):
    spj = nb // 2
    return Step(j * spj + k, (j + nb - k) % nb, j, k, "off" if k else "diag", False, k % SLOTS, k % 2,
                j * (spj - 1) + max(k - 1, 0), j, prev)


def tail_step(q, nb, prev=None):
    spj = nb // 2
    return Step(nb * spj + q, q + spj, q, spj, "off", True, q % SLOTS, q % 2, nb * (spj - 1) + q, nb + q, prev)


def walk(eng, nb, step):
    spj = nb // 2
    step(main_step(0, 0, nb))

    def column(j):
        for k in range(1, spj):
            step(main_step(j, k, nb, main_step(j, k - 1, nb)))

    column(0)
    step(main_step(1, 0, nb, main_step(0, spj - 1, nb)))
    with eng.Fori(1, nb - 1) as j:
        column(j)
        step(main_step(j + 1, 0, nb, main_step(j, spj - 1, nb)))
    column(nb - 1)
    for q in range(spj):
        step(tail_step(q, nb, tail_step(q - 1, nb) if q else main_step(nb - 1, spj - 1, nb)))


def ahead(s, nb):
    spj = nb // 2
    if s.tail:
        return tail_step(s.j + LOOK, nb) if s.j + LOOK < spj else None
    if s.k + LOOK < spj:
        return main_step(s.j, s.k + LOOK, nb)
    if isinstance(s.j, int) and s.j == nb - 1:
        return tail_step(s.k + LOOK - spj, nb)
    return main_step(s.j + 1, s.k + LOOK - spj, nb)


def constants(n):
    eye = np.eye
    ca = np.arange(BLK)
    sub = (ca[:, None] % SUB == np.arange(SUB)).astype(np.float32)
    chan = (ca[:, None] // SUB == np.arange(CH)).astype(np.float32)
    r, o = np.arange(ROWS)[:, None], np.arange(ROWS)[None]
    same_group = (r % CH) // 2 == (o % CH) // 2
    energy = np.array([.5, .5, .5 / n, -.5 / n, .5, .5])
    centre = np.array([.5, 0, .5 / n, -.5 / n, 0, 0])
    f = np.arange(FEATS)
    part = np.arange(BLK)

    def gram_place(first):
        m = np.zeros((BLK, FEATS))
        m[:, first:first + CH] = chan / (4. * n * n)
        return m

    def channel_spread(first):
        m = np.zeros((FEATS, BLK))
        m[first:first + CH] = chan.T / 2
        return m

    pieces = {
        "ident": eye(BLK),
        "sub": sub,
        "one": np.ones((BLK, 1)),
        "chan": chan,
        "mean": np.full((BLK, BLK), 1. / n),
        "gram_s": gram_place(3 * CH),
        "gram_t": gram_place(4 * CH),
        "feat_scale": np.broadcast_to(np.where(f < 3 * CH, 1. / n, -2. / n), (BLK, FEATS)),
        "blocks": ((f[:, None] // CH == f // CH) & (f >= 3 * CH)) | ((f[:, None] < 3 * CH) & (f < 3 * CH)),
        "energy": same_group * energy[r // CH],
        "energy_mean": same_group * centre[r // CH],
        "centre": same_group * centre[r // CH] * (o < 4 * CH),
        "state": np.concatenate([eye(CH, FEATS), eye(CH, FEATS, CH), eye(CH, FEATS, 2 * CH), eye(CH, FEATS, 2 * CH),
                                 eye(CH, FEATS, 3 * CH), eye(CH, FEATS, 4 * CH)]),
        "state_t": np.concatenate([eye(CH, FEATS), eye(CH, FEATS, CH), eye(CH, FEATS, 2 * CH), eye(CH, FEATS, 2 * CH),
                                   eye(CH, FEATS, 3 * CH), eye(CH, FEATS, 4 * CH)]).T,
        "spread_p": channel_spread(3 * CH),
        "spread_q": channel_spread(4 * CH),
        "sub_pairs": np.broadcast_to(eye(SUB).reshape(1, -1), (BLK, SUB * SUB)),
        "keep_mid": np.where((part % 64) // CH >= 1, -1., 0.)[:, None],
        "keep_low": np.where((part % 64) // CH >= 2, -1., 0.)[:, None],
        "onehot": np.broadcast_to(eye(GRP).reshape(1, -1), (BLK, GRP * GRP)),
    }
    where, at = {}, 0
    blob = np.zeros((BLK, sum(v.shape[1] for v in pieces.values())), np.float32)
    for name, v in pieces.items():
        blob[:v.shape[0], at:at + v.shape[1]] = v
        where[name] = (v.shape[0], at, v.shape[1])
        at += v.shape[1]
    pick_channel = np.tile(np.repeat(eye(CH), SUB, axis=1), (3, 1))
    pick_group = np.tile(np.repeat(eye(GRP), BLK, axis=1), (3, 1))
    return blob, where, pick_channel, pick_group


def build(nc, x, weights, biases, const_f32, const_channel, const_group, out, where):
    F32, BF16 = mybir.dt.float32, mybir.dt.bfloat16
    ALU, ACT, AX = mybir.AluOpType, mybir.ActivationFunctionType, mybir.AxisListType
    n = x.shape[2]
    nb = n // BLK
    spj = nb // 2
    steps = nb * spj + spj
    offs = nb * (spj - 1) + spj
    groups = 2 * nb + spj
    ds = bass.ds

    x_rows = x.rearrange("z c (i a) (j b) -> (z i) a c j b", a=BLK, b=BLK)
    x_chan = x.rearrange("z c (i a g) (j b) -> (z c) i a g j b", a=SUB, b=BLK, g=GRP)
    out_rows = out.rearrange("z c (i a) (j b) -> (z i) a c j b", a=BLK, b=BLK)
    out_chan = out.rearrange("z c (i a g) (j b) -> (z c) i a g j b", a=SUB, b=BLK, g=GRP)

    ctx = ExitStack()
    with ctx:
        def sb(name, shape, dt=F32):
            return ctx.enter_context(nc.sbuf_tensor(name, shape, dt))

        def sem(name):
            return ctx.enter_context(nc.semaphore(name))

        TILE = CH * BLK
        xt = sb("xt", [BLK, SLOTS, TILE])
        yt = sb("yt", [BLK, SLOTS, TILE])
        st0 = sb("st0", [BLK, 2, GRP, GW])
        late = sb("late", [BLK, 6 * TILE])
        const = sb("const", [BLK, const_f32.shape[1]])
        both_slots = sb("both_slots", [BLK, max(2 * steps * CH, 2 * n)])
        row_slots = both_slots[:, 0:steps * CH]
        col_slots = both_slots[:, steps * CH:2 * steps * CH]
        shared = sb("shared", [BLK, 2, 4 * BLK])
        jsum, t_sb = shared[:, 0, 0:nb * GRP], shared
        yrow = shared[:, 1, 0:nb * CH]
        gram = sb("gram", [BLK, 2, BLK])
        dia = sb("dia", [BLK, nb, CH])
        lowrank = sb("lowrank", [112, 2, n], BF16)
        colbuf = sb("colbuf", [BLK, 2, max(n, TILE)], BF16)
        colterm = colbuf[0:48, :, 0:n]
        ysum = colbuf[:, :, 0:TILE].bitcast(F32).rearrange("p s w -> p (s w)")
        moving = sb("moving", [112, 2 * 2 * GRP * BLK], BF16)
        wt = sb("wt", [CH, LAYERS, 15, CH])
        bias_sb = sb("bias_sb", [1, LAYERS, 15])
        beta = sb("beta", [1, LAYERS])
        brow = sb("brow", [1, LAYERS, ROWS])
        step_m = sb("step_m", [97, LAYERS, ROWS])
        step_mean = sb("step_mean", [97, LAYERS, ROWS])
        state = sb("state", [ROWS, FEATS + 1])
        state_t = sb("state_t", [FEATS, ROWS])
        mean_row = sb("mean_row", [1, ROWS])
        m80 = sb("m80", [1, 2, FEATS])
        m_col = sb("m_col", [FEATS, 1])
        normed = sb("normed", [97, FEATS + 1])
        means = sb("means", [BLK, 3 * CH])
        rs = sb("rs", [BLK, 2, FEATS])
        phi = sb("phi", [FEATS, FEATS])
        prod = sb("prod", [ROWS, FEATS])
        col = sb("col", [ROWS, 8])
        kron = sb("kron", [BLK, 2, CH, SUB])
        coef = sb("coef", [FEATS, 3, CH])
        coef_b = sb("coef_b", [FEATS, 2, 4, CH])
        krow = sb("krow", [1, 2, 4, CH])
        kd_row = sb("kd_row", [1, CH, SUB])
        ones = sb("ones", [1, 256])
        st1 = late[:, 0:2 * GRP * GW].rearrange("p (s g w) -> p s g w", s=2, g=GRP)
        f1 = late[:, 0:nb * FEATS].rearrange("p (i f) -> p i f", f=FEATS)
        f1s = late[:, nb * FEATS:2 * nb * FEATS].rearrange("p (i f) -> p i f", f=FEATS)
        at_b = 2 * GRP * GW
        wsize = LAYERS * 6 * ROWS
        place = [late[0:CH, at_b + m * wsize:at_b + (m + 1) * wsize].rearrange("p (l r o) -> p l r o", l=LAYERS, r=6)
                 for m in range(2)]
        spread = late[:, at_b:at_b + nb * GRP * SUB].rearrange("p (v a) -> p v a", a=SUB)
        terms = both_slots[0:112, 0:2 * n].rearrange("p (s n) -> p s n", s=2)
        at_c = at_b + 2 * wsize
        coef_d = late[0:FEATS, 3 * TILE:3 * TILE + SUB * BLK].rearrange("f (k c a) -> f k c a", k=SUB, c=CH)
        at_p = 3 * TILE + SUB * BLK
        parts = late[0:112, at_p:at_p + n].bitcast(BF16).rearrange("p (s n) -> p s n", s=2)
        dterm = late[:, 5 * TILE:5 * TILE + n].rearrange("p (v a) -> p v a", a=SUB)
        masked = late[:, at_c:at_c + TILE]
        f2 = late[0:FEATS, 0:3 * n].rearrange("f (i a r g) -> f i a r g", a=SUB, r=3, g=GRP)
        wtmp = late[0:CH, at_c + TILE:at_c + TILE + 4 * LAYERS * CH].rearrange("p (k l o) -> p k l o", k=4, l=LAYERS)
        at_i = at_c + TILE + 4 * LAYERS * CH
        row_i, col_i = (late[:, at_i + m * nb * CH:at_i + (m + 1) * nb * CH].rearrange("p (i c) -> p i c", c=CH)
                        for m in range(2))
        at_y = at_i + max(2 * nb * CH, 8 * BLK // 2)
        yrow_tail = late[:, at_y:at_y + spj * CH]
        gtmp = late[:, at_c:at_c + 2 * BLK].rearrange("p (k w) -> p k w", k=2)
        junk = [(shared[:, ch // 4, 256 + 64 * (ch % 4):320 + 64 * (ch % 4)] if ch < 8
                 else late[:, at_i + 64 * (ch - 8):at_i + 64 * (ch - 7)]).bitcast(BF16) for ch in range(CH)]
        st = [st0, st1]
        out_ij = [late[:, b * TILE:(b + 1) * TILE].rearrange("p (g b) -> p g b", g=GRP) for b in range(2)]
        out_ji = [late[:, (2 + b) * TILE:(3 + b) * TILE].rearrange("p (c a) -> p c a", c=CH) for b in range(2)]
        out_jit = late[:, 4 * TILE:5 * TILE].rearrange("p (q w) -> p q w", q=4)
        ps = ctx.enter_context(nc.psum_tensor("ps", [BLK, 8, 512], F32))

        def c(name):
            rows, at, width = where[name]
            return const[0:rows, at:at + width]

        ident, sub = c("ident"), c("sub")

        x_in = [sem(f"x_in{s}") for s in range(SLOTS)]
        y_in = [sem(f"y_in{s}") for s in range(SLOTS)]
        ident_in = sem("ident_in")
        const_in, weights_in, lowrank_in = sem("const_in"), sem("weights_in"), sem("lowrank_in")
        onehot_set, zeroed = sem("onehot_set"), sem("zeroed")
        place_done, matrices_in, beta_done = sem("place_done"), sem("matrices_in"), sem("beta_done")
        yt_ready, yt_used, st_ready = sem("yt_ready"), sem("yt_used"), sem("st_ready")
        gram_step, gram_used = sem("gram_step"), sem("gram_used")
        rows_done, pool_read, dia_done = sem("rows_done"), sem("pool_read"), sem("dia_done")
        yrows_done = sem("yrows_done")
        pool_own, dve_own = sem("pool_own"), sem("dve_own")
        rows_folded = sem("rows_folded")
        to_pe, from_pe = sem("to_pe"), sem("from_pe")
        f2_ready, f2_done, root_in, root_out = sem("f2_ready"), sem("f2_done"), sem("root_in"), sem("root_out")
        terms_made = sem("terms_made")
        colterm_done, middle_done = sem("colterm_done"), sem("middle_done")
        yt2_ready, yt2_used, moving_ready = sem("yt2_ready"), sem("yt2_used"), sem("moving_ready")
        tmix_ready, mix_ready, t_copied, out_done = sem("tmix_ready"), sem("mix_ready"), sem("t_copied"), sem("out_done")
        diag_own = sem("diag_own")
        jit_turned, ji_copied = sem("jit_turned"), sem("ji_copied")
        ij_stored = [sem(f"ij_stored{b}") for b in range(2)]
        ij_stored_sync = [sem(f"ij_stored_sync{b}") for b in range(2)]
        ji_stored = [sem(f"ji_stored{b}") for b in range(2)]

        def wait(eng, s, value):
            if not (isinstance(value, int) and value <= 0):
                eng.wait_ge(s, value)

        pass1_loads = steps // SLOTS

        def slot_turn(s):
            return s.t // SLOTS if isinstance(s.t, int) else s.j * (spj // SLOTS) + s.k // SLOTS

        def par_turn(s):
            return s.t // 2 if isinstance(s.t, int) else s.j * (spj // 2) + s.k // 2

        def ji_before(s):
            if s.tail:
                return nb * (spj // 2 - 1 + s.par) + s.j // 2
            return s.j * (spj // 2 - 1 + s.par) + (s.k - 1) // 2

        def gram_index(s):
            return nb * 2 + s.j if s.tail else 2 * s.j + (s.kind == "off")

        block = ctx.enter_context(nc.Block())

        @block.sync
        def _(sp):
            sp.dma_start(const[:, 0:BLK], const_f32[:, 0:BLK]).then_inc(ident_in, 16)

            def held(v):
                if not isinstance(v, int):
                    sp.compute_val(v)
                return v

            def load1(s):
                sp.dma_start(yt[:, s.slot].rearrange("p (c b) -> p c b", c=CH),
                             x_rows[s.j, :, :, s.i, :]).then_inc(y_in[s.slot], 16)
                sp.dma_start(xt[:, s.slot].rearrange("p (c b) -> p c b", c=CH),
                             x_rows[s.i, :, :, s.j, :]).then_inc(x_in[s.slot], 16)

            def load2(s):
                sp.dma_start(yt[:, s.slot].rearrange("p (c b) -> p c b", c=CH),
                             x_rows[s.j, :, :, s.i, :]).then_inc(y_in[s.slot], 16)
                for a in range(SUB):
                    sp.dma_start(xt[a:BLK:SUB, s.slot].rearrange("p (g b) -> p g b", g=GRP),
                                 x_chan[:, s.i, a, :, s.j, :]).then_inc(x_in[s.slot], 16)

            first = [main_step(0, k, nb) for k in range(LOOK)]
            for s in first:
                load1(s)
                if s.t == 0:
                    sp.dma_start(const[:, BLK:], const_f32[:, BLK:]).then_inc(const_in, 16)
            for layer in range(LAYERS):
                sp.dma_start(wt[:, layer], weights[layer].rearrange("k c o -> c k o")).then_inc(weights_in, 16)
                sp.dma_start(bias_sb[:, layer], biases[layer].rearrange("(z k) -> z k", z=1)).then_inc(weights_in, 16)
            sp.wait_ge(zeroed, 1)
            for p in range(2):
                for i in range(nb):
                    sp.dma_start(lowrank[0:48, p, i * BLK:(i + 1) * BLK], const_channel).then_inc(lowrank_in, 16)
                for q in range(2):
                    sp.dma_start(moving[64:112, (2 * p + q) * TILE:(2 * p + q + 1) * TILE],
                                 const_group).then_inc(lowrank_in, 16)

            def pass1(s):
                nxt = ahead(s, nb)
                if nxt:
                    nxt = nxt._replace(i=held(nxt.i), j=held(nxt.j))
                t, turned = held(s.t), held(2 * s.t)
                wait(sp, pool_read, nb * spj if s.tail else t)
                if s.tail:
                    wait(sp, yrows_done, nb + s.j if s.j else 0)
                wait(sp, st_ready, t)
                wait(sp, rows_done, t)
                wait(sp, yt_ready, turned)
                if nxt:
                    load1(nxt)
                else:
                    load2(first[s.t + LOOK - steps])

            walk(sp, nb, pass1)
            sp.wait_ge(place_done, 1)
            for m, dst in enumerate((step_m, step_mean)):
                for rb in range(6):
                    sp.dma_start(dst[rb * CH:(rb + 1) * CH], place[m][:, :, rb, :]).then_inc(matrices_in, 16)
            sp.wait_ge(beta_done, 1)
            sp.dma_start(step_mean[96:97], brow[:, :, :]).then_inc(matrices_in, 16)

            def store_ij(s, done):
                i, j = held(s.i), held(s.j)
                sp.wait_ge(out_done, done)
                for a in range(SUB - SP_STORES, SUB):
                    sp.dma_start(out_chan[:, i, a, :, j, :],
                                 out_ij[s.par][a:BLK:SUB]).then_inc(ij_stored_sync[s.par], 16)

            def store_ji(s):
                if s.kind == "off":
                    i, j = held(s.i), held(s.j)
                    wait(sp, ji_copied, held(4 * s.off + 4))
                    sp.dma_start(out_rows[j, :, :, i, :], out_ji[s.par]).then_inc(ji_stored[s.par], 16)

            def pass2(s):
                nxt = ahead(s, nb)
                if not s.prev:
                    sp.wait_ge(st_ready, steps)
                    sp.wait_ge(rows_done, steps)
                    sp.wait_ge(yt_ready, 2 * steps)
                before = held(4 * s.t)
                if nxt:
                    nxt = nxt._replace(i=held(nxt.i), j=held(nxt.j))
                    wait(sp, yt2_used, before)
                    load2(nxt)
                if s.prev:
                    store_ij(s.prev, before)
                    store_ji(s.prev)

            walk(sp, nb, pass2)
            store_ij(tail_step(spj - 1, nb), 4 * steps)
            store_ji(tail_step(spj - 1, nb))
            for b in range(2):
                sp.wait_ge(ij_stored[b], 16 * (SUB - SP_STORES) * steps // 2)
                sp.wait_ge(ij_stored_sync[b], 16 * SP_STORES * steps // 2)
                sp.wait_ge(ji_stored[b], 16 * (nb * (spj // 2 - 1 + b) + spj // 2))

        @block.gpsimd
        def _(pool):
            own = [0]

            def link(ins):
                own[0] += 1
                ins.then_inc(pool_own, 1)
                pool.wait_ge(pool_own, own[0])

            pool.wait_ge(ident_in, 16)
            pool.wait_ge(const_in, 16)
            for b in range(2):
                last = nc.gpsimd.tensor_copy(st[b][:, 0, :, BLK:GW], c("onehot").rearrange("p (g w) -> p g w", g=GRP))
            last.then_inc(onehot_set, 1)
            nc.gpsimd.memset(lowrank[:, :, :], 0.0)
            nc.gpsimd.memset(moving[:, :], 0.0).then_inc(zeroed, 1)

            def masked_diagonal(s):
                pool.wait_ge(x_in[s.slot], 16 * (slot_turn(s) + 1))
                wait(pool, dia_done, s.j)
                nc.gpsimd.tensor_tensor(masked.rearrange("p (c b) -> p c b", c=CH),
                                        xt[:, s.slot].rearrange("p (c b) -> p c b", c=CH),
                                        ident.unsqueeze(1).to_broadcast([BLK, CH, BLK]),
                                        ALU.mult).then_inc(pool_read, 1)

            def add_mirrored(s):
                pool.wait_ge(y_in[s.slot], 16 * (slot_turn(s) + 1))
                pool.wait_ge(pool_read, s.t)
                whole = yt[:, s.slot]
                if s.k == 1:
                    wait(pool, yrows_done, s.j)
                    nc.gpsimd.tensor_tensor(ysum, whole, c("one").to_broadcast([BLK, TILE]),
                                            ALU.mult).then_inc(pool_read, 1)
                else:
                    nc.gpsimd.tensor_tensor(ysum, ysum, whole, ALU.add).then_inc(pool_read, 1)

            def pass1(s):
                if s.kind == "diag":
                    masked_diagonal(s)
                elif not s.tail:
                    add_mirrored(s)

            walk(pool, nb, pass1)

            pool.wait_ge(weights_in, 16 * 2 * LAYERS)
            coefs, mean_coefs = place

            def w(k):
                return wt[:, :, k, :]

            def put(dst, a, b, op=ALU.add):
                link(nc.gpsimd.tensor_tensor(dst, a, b, op))

            def neg(dst, a):
                link(nc.gpsimd.tensor_scalar(dst, a, -1.0, None, ALU.mult))

            link(nc.gpsimd.memset(coefs, 0.0))
            link(nc.gpsimd.memset(mean_coefs, 0.0))
            UR, VR, ER, BR, PR, QR = range(6)
            for rb, (r, s_, d, on_u, on_v) in ((UR, (R_RHO, S_RHO, D_RHO, SAME, SWAP)),
                                               (VR, (R_GAM, S_GAM, D_GAM, SWAP, SAME))):
                put(coefs[:, :, rb, U_], w(r), w(on_u))
                put(coefs[:, :, rb, V_], w(s_), w(on_v))
                put(coefs[:, :, rb, B_], w(r), w(s_))
                put(coefs[:, :, rb, E_], coefs[:, :, rb, B_], w(d))
            tr, ts, td, tk = (wtmp[:, k] for k in range(4))
            for tmp, a, b in ((tr, R_RHO, R_GAM), (ts, S_RHO, S_GAM), (td, D_RHO, D_GAM)):
                put(tmp, w(a), w(b))
            link(nc.gpsimd.tensor_scalar(wtmp[:, 0:3], wtmp[:, 0:3], 1.0 / n, None, ALU.mult))
            link(nc.gpsimd.tensor_scalar(tk, w(ALL_TOTAL), 1.0 / n, None, ALU.mult))
            eb = coefs[:, :, ER]
            bb = coefs[:, :, BR]
            put(eb[:, :, U_], w(R_DIA), tr)
            put(eb[:, :, V_], w(S_DIA), ts)
            put(eb[:, :, B_], eb[:, :, U_], eb[:, :, V_])
            put(eb[:, :, E_], eb[:, :, B_], w(D_DIA))
            put(eb[:, :, E_], eb[:, :, E_], td)
            put(coefs[:, :, PR, P_], w(SAME), w(SWAP))
            put(coefs[:, :, QR, Q_], w(SAME), w(SWAP), ALU.subtract)
            both = coefs[:, :, PR, P_]
            put(eb[:, :, E_], eb[:, :, E_], both)
            neg(bb[:, :, U_], tr)
            neg(bb[:, :, V_], ts)
            put(bb[:, :, E_], bb[:, :, U_], bb[:, :, V_])
            put(bb[:, :, B_], bb[:, :, E_], both)
            put(bb[:, :, E_], bb[:, :, E_], td, ALU.subtract)
            link(nc.gpsimd.tensor_copy(mean_coefs, coefs))
            mb = mean_coefs

            def more(rb, cols, a, op=ALU.add):
                put(mb[:, :, rb, cols], mb[:, :, rb, cols], a, op)

            for rb, r, s_ in ((UR, R_RHO, S_RHO), (VR, R_GAM, S_GAM), (ER, R_DIA, S_DIA)):
                more(rb, U_, w(s_))
                more(rb, V_, w(r))
            for cols in (U_, V_, E_, B_):
                more(UR, cols, w(ALL_TOTAL))
                more(ER, cols, w(ALL_TRACE))
                more(ER, cols, tk)
                more(BR, cols, tk, ALU.subtract)
            more(UR, E_, w(D_TOTAL))
            more(ER, E_, w(D_TRACE))
            more(ER, U_, ts)
            more(ER, V_, tr)
            more(BR, U_, ts, ALU.subtract)
            more(BR, V_, tr, ALU.subtract)
            link(nc.gpsimd.tensor_scalar(td, w(D_TOTAL), 1.0 / n, None, ALU.mult))
            more(ER, E_, td)
            own[0] += 1
            nc.gpsimd.tensor_tensor(mb[:, :, BR, E_], mb[:, :, BR, E_], td, ALU.subtract).then_inc(pool_own, 1)
            pool.wait_ge(pool_own, own[0])
            nc.gpsimd.memset(col[:, 7:8], 0.0).then_inc(place_done, 1)

            pool.wait_ge(rows_done, steps)
            pool.wait_ge(yrows_done, nb + spj)
            slots = row_slots[:, 0:nb * spj * CH].rearrange("p (j k c) -> p j k c", j=nb, k=spj)
            tail = row_slots[:, nb * spj * CH:].rearrange("p (j c) -> p j c", c=CH)
            link(nc.gpsimd.tensor_copy(row_i, slots[:, :, 0]))
            for k in range(1, spj):
                nc.gpsimd.tensor_tensor(row_i[:, 0:nb - k], row_i[:, 0:nb - k], slots[:, k:nb, k], ALU.add)
                link(nc.gpsimd.tensor_tensor(row_i[:, nb - k:nb], row_i[:, nb - k:nb], slots[:, 0:k, k], ALU.add))
            nc.gpsimd.tensor_tensor(row_i[:, spj:nb], row_i[:, spj:nb], tail, ALU.add).then_inc(rows_folded, 1)

            def store_ij(s):
                pool.wait_ge(out_done, 4 * s.t + 4)
                for a in range(SUB - SP_STORES):
                    pool.dma_start(out_chan[:, s.i, a, :, s.j, :],
                                   out_ij[s.par][a:BLK:SUB]).then_inc(ij_stored[s.par], 16)

            walk(pool, nb, store_ij)

        @block.scalar
        def _(act):
            def row_sums(s):
                act.wait_ge(x_in[s.slot], 16 * (slot_turn(s) + 1))
                wait(act, rows_done, s.t)
                if s.tail or s.k == 1:
                    wait(act, yrows_done, nb + s.j if s.tail and s.j else nb - 1 if s.tail else s.j)
                for ch in range(CH):
                    last = nc.scalar.activation(junk[ch], xt[:, s.slot, ch * BLK:(ch + 1) * BLK], ACT.Copy,
                                                accum_out=row_slots[:, ds(s.t * CH + ch, 1)])
                last.then_inc(rows_done, 1)
                if s.prev and not s.prev.tail and (s.kind == "diag" or s.tail):
                    act.wait_ge(rows_done, s.t + 1)
                    act.wait_ge(pool_read, s.t if s.kind == "diag" else nb * spj)
                    mirrored_sums(ysum, yrow, s.prev.j)
                if s.tail:
                    act.wait_ge(rows_done, s.t + 1)
                    act.wait_ge(yrows_done, nb + s.j)
                    act.wait_ge(y_in[s.slot], 16 * (slot_turn(s) + 1))
                    mirrored_sums(yt[:, s.slot], yrow_tail, s.j)

            def mirrored_sums(src, dst, j):
                for ch in range(CH):
                    last = nc.scalar.activation(junk[ch], src[:, ch * BLK:(ch + 1) * BLK], ACT.Copy,
                                                accum_out=dst[:, ds(j * CH + ch, 1)])
                last.then_inc(yrows_done, 1)

            walk(act, nb, row_sums)

            def root(layer):
                act.wait_ge(root_in, layer + 1)
                nc.scalar.activation(col[:, 4:5], col[:, 3:4], ACT.Sqrt).then_inc(root_out, 1)

            root(0)
            act.wait_ge(f2_ready, 1)
            for b in range(n // 512):
                for r in range(3):
                    last = nc.scalar.activation(f2[:, 4 * b:4 * b + 4, :, r].rearrange("f i a g -> f (i a) g"),
                                                ps[0:FEATS, 4 + b].rearrange("f (v g) -> f v g", g=GRP), ACT.Copy)
            last.then_inc(f2_done, 1)
            for layer in range(1, LAYERS):
                root(layer)

            def column_terms(m, j, q):
                base = (m % 2) * (2 * TILE) + q * (TILE // 2)
                last = nc.scalar.activation(
                    moving[0:48, ds(base, TILE // 2)].rearrange("p (g b) -> p g b", g=GRP // 2),
                    colterm[:, q // 2, ds(j * BLK, BLK)].unsqueeze(1).to_broadcast([48, GRP // 2, BLK]), ACT.Copy)
                if q == 3:
                    last.then_inc(moving_ready, 1)

            def more_terms(s, q):
                if s.tail:
                    if s.j == spj - 1:
                        return
                    if q == 0:
                        act.wait_ge(mix_ready, 4 * s.t)
                    column_terms(nb + s.j + 1, s.j + 1, q)
                elif s.k == 1 and not (isinstance(s.j, int) and s.j == 0):
                    if q == 0:
                        act.wait_ge(mix_ready, 4 * spj * s.j)
                    if isinstance(s.j, int):
                        column_terms(nb, 0, q)
                    else:
                        column_terms(s.j + 1, s.j + 1, q)

            def copy_t(s, q):
                idx = 4 * s.t + q
                act.wait_ge(tmix_ready, idx + 1)
                wait(act, out_done, idx - 1)
                nc.scalar.activation(t_sb[:, q % 2], ps[:, 4 + q % 2], ACT.Copy).then_inc(t_copied, 1)

            def copy_ji(s, q):
                if s.kind == "diag":
                    return
                act.wait_ge(jit_turned, 4 * s.off + q + 1)
                wait(act, ji_stored[s.par], 16 * ji_before(s))
                nc.scalar.activation(
                    out_ji[s.par].rearrange("p c (a g) -> p g c a", g=GRP)[:, CG * q:CG * q + CG],
                    ps[:, 6 + q % 2].rearrange("p (g c a) -> p g c a", g=CG, c=CH), ACT.Copy).then_inc(ji_copied, 1)

            def pass2(s):
                for q in range(4):
                    if q or s.prev:
                        copy_t(s if q else s.prev, (q - 1) % 4)
                    if q == 3 or s.prev:
                        copy_ji(s if q == 3 else s.prev, (q - 3) % 4)
                    more_terms(s, q)

            act.wait_ge(lowrank_in, 16 * (2 * nb + 4))
            act.wait_ge(colterm_done, 1)
            for m in range(2):
                for q in range(4):
                    column_terms(m, m, q)
            act.wait_ge(colterm_done, nb // 2)
            walk(act, nb, pass2)
            last_step = tail_step(spj - 1, nb)
            copy_t(last_step, 3)
            for q in range(1, 4):
                copy_ji(last_step, q)
        @block.vector
        def _(dve):
            own = [0]

            def link(ins):
                own[0] += 1
                ins.then_inc(dve_own, 1)
                dve.wait_ge(dve_own, own[0])

            tt = nc.vector.tensor_tensor
            link(nc.vector.memset(gram[:, :, :], 0.0))

            def form(s):
                dve.wait_ge(x_in[s.slot], 16 * (slot_turn(s) + 1))
                wait(dve, gram_step, s.t - 1)
                if isinstance(s.t, int) and s.t == 1:
                    dve.wait_ge(onehot_set, 1)
                for h in range(2):
                    dve.wait_ge(yt_ready, 2 * s.t + h + 1)
                    blk = xt[:, s.slot, h * 1024:(h + 1) * 1024].rearrange("p (c g b) -> p c g b", c=8, g=GRP)
                    mir = ps[:, 2 * h:2 * h + 2].rearrange("p k (c g b) -> p (k c) g b", c=4, g=GRP)
                    for k, op in enumerate((ALU.add, ALU.subtract)):
                        dst = st[s.par][:, k, :, 0:BLK].rearrange("p g (c b) -> p c g b", c=CH)[:, 8 * h:8 * h + 8]
                        last = tt(dst, blk, mir, op)
                    if h:
                        last.then_inc(st_ready, 1)
                    nc.vector.tensor_reduce(col_slots[:, ds(s.t * CH + 8 * h, 8)],
                                            ps[:, 2 * h:2 * h + 2].rearrange("p k (c b) -> p (k c) b", c=4),
                                            AX.X, ALU.add).then_inc(yt_used, 1)

            def take_gram(s):
                g = gram_index(s)
                dve.wait_ge(gram_step, s.t + 1)
                wait(dve, gram_used, g)
                bank = 4 + 2 * (s.par if s.tail else (s.kind == "off"))
                last = nc.vector.scalar_tensor_tensor(gram[:, :, :], ps[:, bank:bank + 2, 0:BLK],
                                                      1.0 if s.kind == "diag" else 2.0, gram[:, :, :],
                                                      ALU.mult, ALU.add)
                if s.kind == "off":
                    part = ps[:, bank, BLK:GW]
                    dst = jsum[:, ds(s.j * GRP, GRP)]
                    last = tt(dst, part, dst, ALU.add) if s.tail else nc.vector.tensor_copy(dst, part)
                last.then_inc(gram_used, 1)

            def ends_group(s):
                return s.kind == "diag" or s.tail or s.k == spj - 1

            def pass1(s):
                form(s)
                if s.prev and ends_group(s.prev):
                    take_gram(s.prev)
                if s.k == 2 and not s.tail:
                    dve.wait_ge(pool_read, s.j * spj + 1)
                    nc.vector.tensor_reduce(dia[:, ds(s.j, 1), :].rearrange("p i c -> p (i c)"),
                                            masked.rearrange("p (c b) -> p c b", c=CH),
                                            AX.X, ALU.add).then_inc(dia_done, 1)

            walk(dve, nb, pass1)

            dve.wait_ge(yt_used, 2 * steps)
            dve.wait_ge(rows_done, steps)
            dve.wait_ge(yrows_done, nb + spj)
            slots = col_slots[:, 0:nb * spj * CH].rearrange("p (j k c) -> p j k c", j=nb, k=spj)
            tail = col_slots[:, nb * spj * CH:].rearrange("p (j c) -> p j c", c=CH)
            link(nc.vector.tensor_copy(col_i, slots[:, :, 0]))
            for k in range(1, spj):
                tt(col_i[:, 0:nb - k], col_i[:, 0:nb - k], slots[:, k:nb, k], ALU.add)
                link(tt(col_i[:, nb - k:nb], col_i[:, nb - k:nb], slots[:, 0:k, k], ALU.add))
            link(tt(col_i[:, spj:nb], col_i[:, spj:nb], tail, ALU.add))
            dve.wait_ge(weights_in, 16 * 2 * LAYERS)
            link(nc.vector.tensor_reduce(beta[:, :], bias_sb[:, :, :], AX.X, ALU.add))
            link(nc.vector.memset(brow[:, :, :], 0.0))
            nc.vector.tensor_copy(brow[:, :, 0:4 * CH],
                                  beta[:, :].unsqueeze(2).to_broadcast([1, LAYERS, 4 * CH])).then_inc(beta_done, 1)
            link(nc.vector.memset(rs[:, :, :], 0.0))
            link(nc.vector.memset(normed[:, :], 0.0))
            nc.vector.memset(normed[96:97, FEATS:FEATS + 1], 1.0)
            nc.vector.memset(ones[:, :], 1.0)
            nc.vector.memset(m80[:, :, :], 0.0)
            link(nc.vector.memset(mean_row[:, :], 0.0))
            take_gram(tail_step(spj - 1, nb))
            dve.wait_ge(gram_used, groups)

            dve.wait_ge(matrices_in, 16 * 13)
            width = nb * GRP
            tt(spread, jsum.unsqueeze(2).to_broadcast([BLK, width, SUB]),
               sub.unsqueeze(1).to_broadcast([BLK, width, SUB]), ALU.mult).then_inc(to_pe, 1)
            link(tt(yrow[:, 0:spj * CH], yrow[:, 0:spj * CH], yrow_tail, ALU.add))
            tt(col_i.rearrange("p i c -> p (i c)"), col_i.rearrange("p i c -> p (i c)"), yrow, ALU.subtract)
            for k in range(2):
                g3 = gtmp[:, k].rearrange("p (c a) -> p c a", c=CH)
                link(tt(g3, gram[:, k].rearrange("p (c a) -> p c a", c=CH),
                        sub.unsqueeze(1).to_broadcast([BLK, CH, SUB]), ALU.mult))
                link(nc.vector.tensor_reduce(rs[:, k, (3 + k) * CH:(4 + k) * CH], g3, AX.X, ALU.add))
            dve.wait_ge(from_pe, 1)
            dve.wait_ge(rows_folded, 1)
            tt(f1[:, :, 0:CH], row_i, yrow.rearrange("p (i c) -> p i c", c=CH), ALU.add)
            link(tt(f1[:, :, CH:2 * CH], col_i, ps[:, 0, 0:nb * CH].rearrange("p (i c) -> p i c", c=CH), ALU.add))
            link(nc.vector.tensor_scalar(f1[:, :, 0:2 * CH], f1[:, :, 0:2 * CH], 1.0 / n, None, ALU.mult))
            dve.wait_ge(dia_done, nb)
            nc.vector.tensor_copy(f1[:, :, 2 * CH:3 * CH], dia[:, :, :]).then_inc(to_pe, 1)
            dve.wait_ge(to_pe, 2)
            dve.wait_ge(from_pe, 2)
            link(nc.vector.tensor_copy(means[:, :], ps[:, 2, 0:3 * CH]))
            for k in range(2):
                nc.vector.tensor_copy(mean_row[:, 2 * k * CH:2 * (k + 1) * CH].rearrange("p (r c) -> p r c", r=2),
                                      means[0:1, 2 * k * CH:(2 * k + 1) * CH].unsqueeze(1).to_broadcast([1, 2, CH]))
            nc.vector.tensor_copy(m80[:, 0, 3 * CH:4 * CH], means[0:1, 0:CH])
            nc.vector.tensor_scalar(m80[:, 1, 3 * CH:4 * CH], means[0:1, 0:CH], -1.0, None, ALU.mult)
            link(tt(f1[:, :, 0:3 * CH], f1[:, :, 0:3 * CH],
                    means[:, :].unsqueeze(1).to_broadcast([BLK, nb, 3 * CH]), ALU.subtract))
            tt(f1[:, :, 3 * CH:4 * CH], f1[:, :, 0:CH], f1[:, :, CH:2 * CH], ALU.add)
            link(tt(f1[:, :, 4 * CH:], f1[:, :, 0:CH], f1[:, :, CH:2 * CH], ALU.subtract))
            link(nc.vector.tensor_scalar(f1[:, :, 3 * CH:], f1[:, :, 3 * CH:], 0.5, None, ALU.mult))
            tt(f1s, f1, c("feat_scale").unsqueeze(1).to_broadcast([BLK, nb, FEATS]),
               ALU.mult).then_inc(to_pe, 1)
            link(nc.vector.tensor_copy(state[:, 0:FEATS], c("state")))
            link(nc.vector.tensor_copy(state_t[:, :], c("state_t")))
            dve.wait_ge(from_pe, 3)
            link(nc.vector.tensor_copy(state[:, FEATS:], ps[0:ROWS, 0, 0:1]))
            link(nc.vector.tensor_copy(m_col[:, :], ps[0:FEATS, 0, 1:2]))
            tt(phi[:, :], ps[0:FEATS, 3, 0:FEATS], c("blocks"), ALU.mult).then_inc(to_pe, 1)
            pe_in, pe_out = 4, 3
            for layer in range(LAYERS):
                dve.wait_ge(from_pe, pe_out + 1)
                link(tt(col[:, 0:1], state[:, FEATS:], ps[0:ROWS, 0, 0:1], ALU.subtract))
                link(tt(col[:, 1:2], col[:, 0:1], col[:, 0:1], ALU.mult))
                link(tt(prod[:, :], state[:, 0:FEATS], ps[0:ROWS, 1, 0:FEATS], ALU.mult))
                nc.vector.tensor_reduce(col[:, 2:3], prod[:, :], AX.X, ALU.add).then_inc(to_pe, 1)
                dve.wait_ge(from_pe, pe_out + 2)
                nc.vector.tensor_scalar(col[:, 3:4], ps[0:ROWS, 2, 0:1], EPS, None, ALU.add).then_inc(root_in, 1)
                dve.wait_ge(root_out, layer + 1)
                link(nc.vector.reciprocal(col[:, 5:6], col[:, 4:5]))
                link(tt(col[:, 2:3], col[:, 5:6], col[:, 5:6], ALU.mult))
                link(tt(col[:, 2:3], col[:, 2:3], col[:, 3:4], ALU.mult))
                link(nc.vector.tensor_scalar(col[:, 2:3], col[:, 2:3], -0.5, 1.5, ALU.mult, ALU.add))
                link(tt(col[:, 5:6], col[:, 5:6], col[:, 2:3], ALU.mult))
                nc.vector.tensor_scalar(normed[0:ROWS, 0:FEATS], state[:, 0:FEATS], col[:, 5:6], None, ALU.mult)
                tt(normed[0:ROWS, FEATS:], col[:, 0:1], col[:, 5:6], ALU.mult).then_inc(to_pe, 1)
                dve.wait_ge(from_pe, pe_out + 3)
                tt(state[:, :], state[:, :], ps[0:ROWS, 3, 0:FEATS + 1], ALU.add)
                tt(mean_row[:, :], mean_row[:, :], ps[0:1, 2, 256:256 + ROWS], ALU.add)
                tt(state_t[:, :], state_t[:, :], ps[0:FEATS, 0, 256:256 + ROWS], ALU.add).then_inc(to_pe, 1)
                pe_in, pe_out = pe_in + 3, pe_out + 3
            dve.wait_ge(to_pe, pe_in)
            link(tt(coef[:, 0], state_t[:, U_], state_t[:, V_], ALU.add))
            link(tt(coef[:, 1], state_t[:, U_], state_t[:, V_], ALU.subtract))
            link(nc.vector.tensor_scalar(coef[:, 0:2], coef[:, 0:2], 0.5, None, ALU.mult))
            tt(coef[:, 0:2], coef[:, 0:2], state_t[:, 4 * CH:].rearrange("p (k c) -> p k c", k=2), ALU.subtract)
            link(tt(coef[:, 2], state_t[:, E_], state_t[:, B_], ALU.subtract))
            nc.vector.tensor_copy(coef_b[:, 0], coef[:, 0].unsqueeze(1).to_broadcast([FEATS, 4, CH]))
            nc.vector.tensor_scalar(coef_b[:, 1], coef[:, 1].unsqueeze(1).to_broadcast([FEATS, 4, CH]),
                                    -1.0, None, ALU.mult)
            for a in range(SUB):
                tt(coef_d[:, a], coef[:, 2].unsqueeze(2).to_broadcast([FEATS, CH, SUB]),
                   c("sub_pairs")[0:FEATS, a * SUB:(a + 1) * SUB].unsqueeze(1).to_broadcast([FEATS, CH, SUB]), ALU.mult)
            link(tt(krow[:, 1, 0], mean_row[:, E_], mean_row[:, B_], ALU.subtract))
            nc.vector.tensor_copy(kd_row[:, :, :], krow[:, 1, 0].unsqueeze(2).to_broadcast([1, CH, SUB]))
            dve.wait_ge(from_pe, pe_out + 1)
            link(tt(krow[:, 1, 1], mean_row[:, U_], ps[0:1, 2, 0:CH], ALU.subtract))
            nc.vector.tensor_copy(krow[:, 0], krow[:, 1, 1].unsqueeze(1).to_broadcast([1, 4, CH]))
            for k in range(2):
                last = tt(kron[:, k], ps[:, k, 0:CH].unsqueeze(2).to_broadcast([BLK, CH, SUB]),
                          sub.unsqueeze(1).to_broadcast([BLK, CH, SUB]), ALU.mult)
            last.then_inc(to_pe, 1)
            dve.wait_ge(from_pe, pe_out + 2)
            tt(dterm, ps[:, 3, 0:width].unsqueeze(2).to_broadcast([BLK, width, SUB]),
               sub.unsqueeze(1).to_broadcast([BLK, width, SUB]), ALU.mult).then_inc(to_pe, 1)
            dve.wait_ge(lowrank_in, 16 * (2 * nb + 4))
            dve.wait_ge(rows_folded, 1)
            for b in range(nb // 2):
                dve.wait_ge(terms_made, b + 1)
                whole = ps[0:112, b].rearrange("p (s n) -> p s n", s=2)
                part = parts[:, :, b * 256:(b + 1) * 256]
                rest = terms[:, :, b * 256:(b + 1) * 256]
                link(nc.vector.tensor_copy(part, whole))
                link(nc.vector.scalar_tensor_tensor(rest, part, c("keep_mid")[0:112], whole, ALU.mult, ALU.add))
                link(nc.vector.tensor_copy(part, rest))
                nc.vector.scalar_tensor_tensor(colterm[:, :, b * 256:(b + 1) * 256], part[0:48], c("keep_low")[0:48],
                                               rest[0:48], ALU.mult, ALU.add).then_inc(colterm_done, 1)
                nc.vector.scalar_tensor_tensor(lowrank[64:112, :, b * 256:(b + 1) * 256], part[64:112],
                                               c("keep_low")[64:112], rest[64:112],
                                               ALU.mult, ALU.add).then_inc(middle_done, 1)
            dve.wait_ge(middle_done, nb // 2)
            dve.wait_ge(colterm_done, nb // 2)

            def form2(s, q):
                idx = 4 * s.t + q
                if q == 0:
                    dve.wait_ge(x_in[s.slot], 16 * (pass1_loads + SUB * (slot_turn(s) + 1)))
                dve.wait_ge(yt2_ready, idx + 1)
                wait(dve, mix_ready, idx - 3)
                for k, op in enumerate((ALU.add, ALU.subtract)):
                    last = tt(st0[:, k, CG * q:CG * q + CG, 0:BLK],
                              xt[:, s.slot, q * 512:(q + 1) * 512].rearrange("p (g b) -> p g b", g=CG),
                              ps[:, q % 2].rearrange("p (g b) -> p g b", g=CG), op)
                last.then_inc(yt2_used, 1)

            def combine(s, q):
                idx = 4 * s.t + q
                dve.wait_ge(mix_ready, idx + 1)
                dve.wait_ge(t_copied, idx + 1)
                if q == 0:
                    wait(dve, ij_stored[s.par], 16 * (SUB - SP_STORES) * par_turn(s))
                    wait(dve, ij_stored_sync[s.par], 16 * SP_STORES * par_turn(s))
                s_prod = ps[:, 2 + q % 2].rearrange("p (g b) -> p g b", g=CG)
                t_prod = t_sb[:, q % 2].rearrange("p (g b) -> p g b", g=CG)
                dst = out_ij[s.par][:, CG * q:CG * q + CG]
                first = tt(dst, s_prod, t_prod, ALU.add)
                if s.kind == "diag":
                    last = first
                    if q == 3:
                        first.then_inc(diag_own, 1)
                        wait(dve, jit_turned, 4 * s.off)
                        dve.wait_ge(diag_own, s.j + 1)
                        at = s.par * TILE
                        span = late[:, at:at + GRP * (BLK + 1)].rearrange("p (g w) -> p g w", g=GRP)[:, :, 0:BLK:GRP]
                        last = tt(span, span, dterm[:, ds(s.j * GRP, GRP), :], ALU.add)
                else:
                    if s.k > 1:
                        dve.wait_ge(jit_turned, 4 * s.off + q - 3)
                    last = tt(out_jit[:, q].rearrange("p (g b) -> p g b", g=CG), s_prod, t_prod, ALU.subtract)
                last.then_inc(out_done, 1)

            def pass2(s):
                for q in range(4):
                    form2(s, q)
                    if q >= 2 or s.prev:
                        combine(s if q >= 2 else s.prev, (q - 2) % 4)

            walk(dve, nb, pass2)
            for q in (2, 3):
                combine(tail_step(spj - 1, nb), q)

        @block.tensor
        def _(pe):
            mm = nc.tensor.matmul
            pe.wait_ge(ident_in, 16)

            def turn(s):
                pe.wait_ge(y_in[s.slot], 16 * (slot_turn(s) + 1))
                for h in range(2):
                    wait(pe, yt_used, 2 * s.t + h - 1)
                    for ch in range(8 * h, 8 * h + 8):
                        last = nc.tensor.transpose(ps[:, ch // 4, (ch % 4) * BLK:(ch % 4 + 1) * BLK],
                                                   yt[:, s.slot, ch * BLK:(ch + 1) * BLK], ident)
                    last.then_inc(yt_ready, 1)

            def grams(s):
                g = gram_index(s)
                opens = s.kind == "diag" or s.tail or s.k == 1
                closes = s.kind == "diag" or s.tail or s.k == spj - 1
                bank = 4 + 2 * (s.par if s.tail else (s.kind == "off"))
                pe.wait_ge(st_ready, s.t + 1)
                if opens and s.kind == "off":
                    pe.wait_ge(gram_used, g - 1)
                for k in range(2):
                    width = BLK if s.kind == "diag" or k else GW
                    for grp in range(GRP):
                        last = mm(ps[:, bank + k, 0:width], st[s.par][:, k, grp, 0:BLK], st[s.par][:, k, grp, 0:width],
                                  start=opens and grp == 0, stop=closes and grp == GRP - 1)
                last.then_inc(gram_step, 1)

            def pass1(s):
                turn(s)
                if s.prev:
                    grams(s.prev)

            walk(pe, nb, pass1)
            grams(tail_step(spj - 1, nb))

            one = ones[0:1, 0:1]
            pe.wait_ge(const_in, 16)
            pe.wait_ge(gram_used, groups)
            pe.wait_ge(to_pe, 1)
            for i in range(nb):
                last = mm(ps[:, 0, i * CH:(i + 1) * CH], spread[:, i * GRP:(i + 1) * GRP].rearrange("p g a -> p (g a)"),
                          c("chan"), start=True, stop=True)
            last.then_inc(from_pe, 1)
            pe.wait_ge(to_pe, 2)
            for i in range(nb):
                last = mm(ps[:, 2, 0:3 * CH], c("mean"), f1[:, i, 0:3 * CH], start=i == 0, stop=i == nb - 1)
            last.then_inc(from_pe, 1)
            pe.wait_ge(to_pe, 3)
            mm(ps[0:ROWS, 0, 0:1], mean_row[:, :], one, start=True, stop=True)
            mm(ps[0:FEATS, 0, 1:2], m80[:, 0], one, start=True, stop=True)
            cov = ps[0:FEATS, 3, 0:FEATS]
            for i in range(nb):
                mm(cov, f1s[:, i], f1[:, i], start=i == 0, stop=False)
            mm(cov, c("gram_s"), rs[:, 0], start=False, stop=False)
            mm(cov, c("gram_t"), rs[:, 1], start=False, stop=False)
            mm(cov, m80[:, 1], m80[:, 0], start=False, stop=True).then_inc(from_pe, 1)
            for i in range(nb):
                last = nc.tensor.transpose(ps[0:FEATS, 4 + i // 4, (i % 4) * BLK:(i % 4 + 1) * BLK], f1[:, i], ident)
            last.then_inc(f2_ready, 1)
            pe_in = 4
            for layer in range(LAYERS):
                pe.wait_ge(to_pe, pe_in)
                mm(ps[0:ROWS, 0, 0:1], c("centre"), state[:, FEATS:], start=True, stop=True)
                mm(ps[0:ROWS, 1, 0:FEATS], state_t[:, :], phi[:, :], start=True, stop=True).then_inc(from_pe, 1)
                pe.wait_ge(to_pe, pe_in + 1)
                mm(ps[0:ROWS, 2, 0:1], c("energy"), col[:, 2:3], start=True, stop=False)
                mm(ps[0:ROWS, 2, 0:1], c("energy_mean"), col[:, 1:2], start=False, stop=True).then_inc(from_pe, 1)
                pe.wait_ge(to_pe, pe_in + 2)
                mm(ps[0:ROWS, 3, 0:FEATS], step_m[0:ROWS, layer], normed[0:ROWS, 0:FEATS], start=True, stop=True)
                mm(ps[0:ROWS, 3, FEATS:FEATS + 1], step_mean[:, layer], normed[:, FEATS:], start=True, stop=True)
                mm(ps[0:1, 2, 256:256 + ROWS], normed[:, FEATS:], step_mean[:, layer], start=True, stop=True)
                mm(ps[0:FEATS, 0, 256:256 + ROWS], normed[0:ROWS, 0:FEATS], step_m[0:ROWS, layer],
                   start=True, stop=True).then_inc(from_pe, 1)
                pe_in += 3
            pe.wait_ge(to_pe, pe_in)
            mm(ps[:, 0, 0:CH], c("spread_p"), state_t[:, P_], start=True, stop=True)
            mm(ps[:, 1, 0:CH], c("spread_q"), state_t[:, Q_], start=True, stop=True)
            mm(ps[0:1, 2, 0:CH], m_col[:, :], state_t[:, P_], start=True, stop=True).then_inc(from_pe, 1)
            pe.wait_ge(to_pe, pe_in + 1)
            pe.wait_ge(f2_done, 1)
            for a in range(SUB):
                mm(ps[:, 3, 0:nb * GRP], coef_d[:, a].rearrange("f c a -> f (c a)"), f2[:, :, a, 0],
                   start=a == 0, stop=False)
            mm(ps[:, 3, 0:nb * GRP], kd_row[:, :, :].rearrange("z c a -> z (c a)"), ones[:, 0:nb * GRP],
               start=False, stop=True).then_inc(from_pe, 1)
            for b in range(nb // 2):
                if b == 3:
                    pe.wait_ge(to_pe, pe_in + 2)
                for k in range(2):
                    dst = ps[0:64, b, k * 256:(k + 1) * 256]
                    mm(dst, coef_b[:, k].rearrange("f r c -> f (r c)"),
                       f2[:, 2 * b:2 * b + 2, :, 0].rearrange("f i a g -> f (i a) g"), start=True, stop=k == 1)
                    if k == 0:
                        mm(dst, krow[:, 0].rearrange("z r c -> z (r c)"), ones[:, :], start=False, stop=True)
                for i2 in range(2):
                    dst = ps[64:112, b].rearrange("p (k i c a) -> p i a k c", k=2, i=2, c=CH)
                    for a in range(SUB):
                        last = mm(dst[:, i2, a], f2[:, 2 * b + i2, a].rearrange("f r g -> f (r g)"),
                                  coef[:, 0:2], start=True, stop=True)
                last.then_inc(terms_made, 1)
            pe.wait_ge(middle_done, 2)

            def turn2(s, q):
                if q == 0:
                    pe.wait_ge(y_in[s.slot], 16 * (pass1_loads + slot_turn(s) + 1))
                wait(pe, yt2_used, 4 * s.t + q - 1)
                rows = yt[:, s.slot].rearrange("p (v g) -> p g v", g=GRP)
                for g in range(CG):
                    last = nc.tensor.transpose(ps[:, q % 2, g * BLK:(g + 1) * BLK], rows[:, CG * q + g], ident)
                last.then_inc(yt2_ready, 1)

            def mix(s, q):
                idx = 4 * s.t + q
                pe.wait_ge(yt2_used, idx + 1)
                pe.wait_ge(moving_ready, s.group + 1)
                wait(pe, out_done, idx - 1)
                base = (s.group % 2) * (2 * TILE)
                for k, done in ((1, tmix_ready), (0, mix_ready)):
                    dst = ps[:, 2 + 2 * k + q % 2]
                    mm(dst, lowrank[:, k, ds(s.i * BLK, BLK)], moving[:, ds(base + k * TILE + q * 512, 512)],
                       start=True, stop=False)
                    mm(dst, kron[:, k].rearrange("p c a -> p (c a)"), st0[:, k, CG * q:CG * q + CG, 0:BLK],
                       start=False, stop=True).then_inc(done, 1)

            def turn_back(s, q):
                if s.kind == "diag":
                    if q == 3:
                        wait(pe, ji_copied, 4 * s.off)
                    return
                pe.wait_ge(out_done, 4 * s.t + q + 1)
                if s.k > 1 or q > 1:
                    pe.wait_ge(ji_copied, 4 * s.off + q - 1)
                for g in range(CG):
                    last = nc.tensor.transpose(ps[:, 6 + q % 2, g * BLK:(g + 1) * BLK],
                                               out_jit[:, q, g * BLK:(g + 1) * BLK], ident)
                last.then_inc(jit_turned, 1)

            def pass2(s):
                for q in range(4):
                    turn2(s, q)
                    if q or s.prev:
                        mix(s if q else s.prev, (q - 1) % 4)
                    if q == 3 or s.prev:
                        turn_back(s if q == 3 else s.prev, (q - 3) % 4)

            walk(pe, nb, pass2)
            last_step = tail_step(spj - 1, nb)
            mix(last_step, 3)
            for q in range(1, 4):
                turn_back(last_step, q)


def kernel(x, **inputs):
    import concourse.bacc as bacc
    from concourse.bass_utils import run_bass_kernel_spmd

    nc = bacc.Bacc("TRN2", target_bir_lowering=False, num_devices=1)
    arrays, aps = {}, {}

    def dram(name, a):
        arrays[name] = a
        aps[name] = nc.dram_tensor(name, a.shape, mybir.dt.from_np(a.dtype), kind="ExternalInput").ap()
        return aps[name]

    blob, where, pick_channel, pick_group = constants(x.shape[2])
    bf16 = mybir.dt.np(mybir.dt.bfloat16)
    xin = dram("x", np.ascontiguousarray(x))
    ws = [dram(f"weights{k}", np.ascontiguousarray(inputs[f"L{k}_conv_weights"])) for k in range(LAYERS)]
    bs = [dram(f"bias{k}", np.ascontiguousarray(inputs[f"L{k}_conv_bias"])) for k in range(LAYERS)]
    cf = dram("const_f32", blob)
    cc = dram("const_channel", pick_channel.astype(bf16))
    cg = dram("const_group", pick_group.astype(bf16))
    out = nc.dram_tensor("out", x.shape, mybir.dt.float32, kind="ExternalOutput").ap()
    build(nc, xin, ws, bs, cf, cc, cg, out, where)
    r = run_bass_kernel_spmd(nc, [arrays], core_ids=[0])
    return r.results[0]["out"]
```
